# Optimizing a Trainium2 kernel written in Bass

```python
import numpy as np
import jax
import jax.numpy as jnp

def _softmax(x, axis=-1):
    return jax.nn.softmax(x, axis=axis)

def _gelu(x):
    return jax.nn.gelu(x, approximate=True)

def _silu(x):
    return jax.nn.silu(x)

def _sigmoid(x):
    return jax.nn.sigmoid(x)

def _layernorm(x, axis=-1, eps=1e-05):
    m = jnp.mean(x, axis=axis, keepdims=True)
    v = jnp.var(x, axis=axis, keepdims=True)
    return (x - m) / jnp.sqrt(v + eps)

def _scatter_add(tgt, idx, src, axis=0):
    return tgt.at[idx].add(src)

def _segment_sum(src, seg, n):
    return jax.ops.segment_sum(src, seg, n)
kernel_name = 'mk_dlrm_tower_d1_rec_r8_94078c'

def setup_inputs(seed: int=0):
    np.random.seed(seed)
    _w = jnp.asarray

    def _rec_inputs():
        import jax
        import jax.numpy as jnp
        _tk = jax.random.key(seed)
        ids = jnp.stack([jax.random.randint(jax.random.fold_in(_tk, 200 + f), (2048,), 0, v, jnp.int32) for f, v in enumerate([1250, 1000, 1000, 1000, 125000, 12500, 1000, 1000, 1000, 1000, 12500, 12500, 12500, 12500, 1000, 12500, 1250, 1250, 1000, 1250, 12500, 1250, 12500, 1250, 1250, 1000])], axis=1)
        tbl_0 = 0.05 * jax.random.normal(jax.random.fold_in(_tk, 500 + 0), (1250, 128), jnp.float32)
        tbl_1 = 0.05 * jax.random.normal(jax.random.fold_in(_tk, 500 + 1), (1000, 128), jnp.float32)
        tbl_2 = 0.05 * jax.random.normal(jax.random.fold_in(_tk, 500 + 2), (1000, 128), jnp.float32)
        tbl_3 = 0.05 * jax.random.normal(jax.random.fold_in(_tk, 500 + 3), (1000, 128), jnp.float32)
        tbl_4 = 0.05 * jax.random.normal(jax.random.fold_in(_tk, 500 + 4), (125000, 128), jnp.float32)
        tbl_5 = 0.05 * jax.random.normal(jax.random.fold_in(_tk, 500 + 5), (12500, 128), jnp.float32)
        tbl_6 = 0.05 * jax.random.normal(jax.random.fold_in(_tk, 500 + 6), (1000, 128), jnp.float32)
        tbl_7 = 0.05 * jax.random.normal(jax.random.fold_in(_tk, 500 + 7), (1000, 128), jnp.float32)
        tbl_8 = 0.05 * jax.random.normal(jax.random.fold_in(_tk, 500 + 8), (1000, 128), jnp.float32)
        tbl_9 = 0.05 * jax.random.normal(jax.random.fold_in(_tk, 500 + 9), (1000, 128), jnp.float32)
        tbl_10 = 0.05 * jax.random.normal(jax.random.fold_in(_tk, 500 + 10), (12500, 128), jnp.float32)
        tbl_11 = 0.05 * jax.random.normal(jax.random.fold_in(_tk, 500 + 11), (12500, 128), jnp.float32)
        tbl_12 = 0.05 * jax.random.normal(jax.random.fold_in(_tk, 500 + 12), (12500, 128), jnp.float32)
        tbl_13 = 0.05 * jax.random.normal(jax.random.fold_in(_tk, 500 + 13), (12500, 128), jnp.float32)
        tbl_14 = 0.05 * jax.random.normal(jax.random.fold_in(_tk, 500 + 14), (1000, 128), jnp.float32)
        tbl_15 = 0.05 * jax.random.normal(jax.random.fold_in(_tk, 500 + 15), (12500, 128), jnp.float32)
        tbl_16 = 0.05 * jax.random.normal(jax.random.fold_in(_tk, 500 + 16), (1250, 128), jnp.float32)
        tbl_17 = 0.05 * jax.random.normal(jax.random.fold_in(_tk, 500 + 17), (1250, 128), jnp.float32)
        tbl_18 = 0.05 * jax.random.normal(jax.random.fold_in(_tk, 500 + 18), (1000, 128), jnp.float32)
        tbl_19 = 0.05 * jax.random.normal(jax.random.fold_in(_tk, 500 + 19), (1250, 128), jnp.float32)
        tbl_20 = 0.05 * jax.random.normal(jax.random.fold_in(_tk, 500 + 20), (12500, 128), jnp.float32)
        tbl_21 = 0.05 * jax.random.normal(jax.random.fold_in(_tk, 500 + 21), (1250, 128), jnp.float32)
        tbl_22 = 0.05 * jax.random.normal(jax.random.fold_in(_tk, 500 + 22), (12500, 128), jnp.float32)
        tbl_23 = 0.05 * jax.random.normal(jax.random.fold_in(_tk, 500 + 23), (1250, 128), jnp.float32)
        tbl_24 = 0.05 * jax.random.normal(jax.random.fold_in(_tk, 500 + 24), (1250, 128), jnp.float32)
        tbl_25 = 0.05 * jax.random.normal(jax.random.fold_in(_tk, 500 + 25), (1000, 128), jnp.float32)
        _rk = jax.random.fold_in(_tk, 7)
        r_dense_features = -0.000292821 + 1.00034 * jax.random.normal(jax.random.fold_in(_rk, 101), (2048, 128), jnp.float32)
        W_top1 = 0.0405887 * jax.random.normal(jax.random.fold_in(_tk, 801), (607, 512), jnp.float32)
        W_top2 = 0.0441942 * jax.random.normal(jax.random.fold_in(_tk, 802), (512, 256), jnp.float32)
        W_top3 = 0.0625 * jax.random.normal(jax.random.fold_in(_tk, 803), (256, 1), jnp.float32)
        b_top1 = jnp.zeros((512,), jnp.float32)
        b_top2 = jnp.zeros((256,), jnp.float32)
        return (r_dense_features, ids, tbl_0, tbl_1, tbl_2, tbl_3, tbl_4, tbl_5, tbl_6, tbl_7, tbl_8, tbl_9, tbl_10, tbl_11, tbl_12, tbl_13, tbl_14, tbl_15, tbl_16, tbl_17, tbl_18, tbl_19, tbl_20, tbl_21, tbl_22, tbl_23, tbl_24, tbl_25, W_top1, b_top1, W_top2, b_top2, W_top3)
    r_dense_features, ids, tbl_0, tbl_1, tbl_2, tbl_3, tbl_4, tbl_5, tbl_6, tbl_7, tbl_8, tbl_9, tbl_10, tbl_11, tbl_12, tbl_13, tbl_14, tbl_15, tbl_16, tbl_17, tbl_18, tbl_19, tbl_20, tbl_21, tbl_22, tbl_23, tbl_24, tbl_25, W_top1, b_top1, W_top2, b_top2, W_top3 = _rec_inputs()

    def _L0_rec_setup():
        import jax, jax.numpy as jnp
        import numpy as np
        F = 26
        _TRIU_I, _TRIU_J = np.triu_indices(F + 1, k=1)
        key = jax.random.key(seed)
        k1, k2 = jax.random.split(key)
        B, D = (4096, 128)
        dense_features = jax.random.normal(k1, (B, D), dtype=jnp.float32)
        sparse_features = jax.random.normal(k2, (B, F, D), dtype=jnp.float32)
        return {'dense_features': dense_features, 'sparse_features': sparse_features}
    _L0_rec_all = _L0_rec_setup()
    _L0_rec_in = {k: v for k, v in _L0_rec_all.items() if k in ()}
    del _L0_rec_all
    return {'r_dense_features': r_dense_features, 'ids': ids, 'tbl_0': tbl_0, 'tbl_1': tbl_1, 'tbl_2': tbl_2, 'tbl_3': tbl_3, 'tbl_4': tbl_4, 'tbl_5': tbl_5, 'tbl_6': tbl_6, 'tbl_7': tbl_7, 'tbl_8': tbl_8, 'tbl_9': tbl_9, 'tbl_10': tbl_10, 'tbl_11': tbl_11, 'tbl_12': tbl_12, 'tbl_13': tbl_13, 'tbl_14': tbl_14, 'tbl_15': tbl_15, 'tbl_16': tbl_16, 'tbl_17': tbl_17, 'tbl_18': tbl_18, 'tbl_19': tbl_19, 'tbl_20': tbl_20, 'tbl_21': tbl_21, 'tbl_22': tbl_22, 'tbl_23': tbl_23, 'tbl_24': tbl_24, 'tbl_25': tbl_25, 'W_top1': W_top1, 'b_top1': b_top1, 'W_top2': W_top2, 'b_top2': b_top2, 'W_top3': W_top3}

def reference(r_dense_features, ids, tbl_0, tbl_1, tbl_2, tbl_3, tbl_4, tbl_5, tbl_6, tbl_7, tbl_8, tbl_9, tbl_10, tbl_11, tbl_12, tbl_13, tbl_14, tbl_15, tbl_16, tbl_17, tbl_18, tbl_19, tbl_20, tbl_21, tbl_22, tbl_23, tbl_24, tbl_25, W_top1, b_top1, W_top2, b_top2, W_top3):
    import jax
    import jax.numpy as jnp

    def _L0_rec_ref(dense_features, sparse_features):
        import jax, jax.numpy as jnp
        import numpy as np
        F = 26
        _TRIU_I, _TRIU_J = np.triu_indices(F + 1, k=1)
        combined = jnp.concatenate([dense_features[:, None, :], sparse_features], axis=1)
        interactions = jnp.einsum('bfd,bgd->bfg', combined, combined)
        interactions_flat = interactions[:, _TRIU_I, _TRIU_J]
        return jnp.concatenate([dense_features, interactions_flat], axis=1)
    e = jnp.stack([tbl_0[ids[:, 0]], tbl_1[ids[:, 1]], tbl_2[ids[:, 2]], tbl_3[ids[:, 3]], tbl_4[ids[:, 4]], tbl_5[ids[:, 5]], tbl_6[ids[:, 6]], tbl_7[ids[:, 7]], tbl_8[ids[:, 8]], tbl_9[ids[:, 9]], tbl_10[ids[:, 10]], tbl_11[ids[:, 11]], tbl_12[ids[:, 12]], tbl_13[ids[:, 13]], tbl_14[ids[:, 14]], tbl_15[ids[:, 15]], tbl_16[ids[:, 16]], tbl_17[ids[:, 17]], tbl_18[ids[:, 18]], tbl_19[ids[:, 19]], tbl_20[ids[:, 20]], tbl_21[ids[:, 21]], tbl_22[ids[:, 22]], tbl_23[ids[:, 23]], tbl_24[ids[:, 24]], tbl_25[ids[:, 25]]], axis=1)
    z = _L0_rec_ref(r_dense_features, e)
    z = z.reshape(z.shape[0], -1)
    h = jnp.concatenate([z, r_dense_features], axis=1)
    h = jnp.maximum(h @ W_top1 + b_top1, 0.0)
    h = jnp.maximum(h @ W_top2 + b_top2, 0.0)
    y = h @ W_top3
    return y

_drawn_inputs = setup_inputs


def setup_inputs(seed=0):
    import zlib

    import numpy as np

    out = dict(_drawn_inputs(seed))
    spreads = {'b_top1': (0.0, 0.1), 'b_top2': (0.0, 0.1)}
    factors = {}
    for name, (base, spread) in spreads.items():
        noise = np.random.default_rng([zlib.crc32(name.encode()), seed]).standard_normal(out[name].shape)
        drawn = base * np.exp(spread * noise) if base else spread * noise
        out[name] = jnp.asarray(drawn.astype(out[name].dtype))
    for name, factor in factors.items():
        out[name] = (out[name] * factor).astype(out[name].dtype)
    return out
```

```python
from contextlib import ExitStack

import numpy as np

import concourse.bass as bass
from concourse import mybir

F32 = mybir.dt.float32
F32R = mybir.dt.float32r
I32 = mybir.dt.int32
ALU = mybir.AluOpType
ACT = mybir.ActivationFunctionType

P = 128
D = 128
GROUP = 2 * P
ONEHOT = 7
QUAD = 4
BLOCK = 32
BANK = 512


def feature_order(rows):
    small = sorted(sorted(range(len(rows)), key=lambda f: (rows[f], f))[:ONEHOT])
    return [f for f in range(len(rows)) if f not in small], small


def pair_chunks(slots):
    return -(-(slots - 1) // QUAD)


def build_tower(nc, dense, ids, onehot_ids, tables, w1, b1, w2, b2, w3, y_out):
    SAMPLES = dense.shape[0]
    GROUPS = SAMPLES // GROUP
    NF = len(tables)
    SLOTS = NF + 1
    gathered_f, onehot_f = feature_order([t.shape[0] for t in tables])
    NX = 1 + len(gathered_f)
    PER = BANK // P
    BATCHES = [list(range(x, min(x + PER, NX))) for x in range(0, NX, PER)]
    NT = len(BATCHES)
    NB = 2 * NT
    TABLE_ROWS = tables[onehot_f[0]].shape[0]
    assert all(tables[f].shape[0] == TABLE_ROWS for f in onehot_f)
    RC = 8
    RP = TABLE_ROWS // RC
    assert RP * RC == TABLE_ROWS and RP <= P
    HALVES = 2 * len(onehot_f)
    NO = -(-len(onehot_f) // 2)
    PC = pair_chunks(SLOTS)
    KC = PC + 1
    H1, H2 = w1.shape[2], w2.shape[1]
    M1, M2 = H1 // P, H2 // P
    NG = SLOTS - 1
    RUNS = P // QUAD
    PARTS = 4
    IP = RUNS // PARTS
    assert NO % 2 == 0 and M1 == 4 and IP * QUAD * NG <= 2 * BANK and BLOCK * QUAD == P

    BESIDE = {
        0: [("old", 0), ("old", 1)],
        1: [("old", 2), ("old", 3)],
        2: [("onehot", 0)],
        3: [("onehot", 1)],
        4: [("onehot", 2)],
        5: [("onehot", 3), ("layer1", 0)],
        6: [("layer1", 1), ("new", 0)],
        7: [("layer1", 2), ("new", 1)],
        8: [("layer1", 3), ("new", 2), ("new", 3), ("layer2", 0)],
        9: [("layer3", 0)],
    }
    BESIDE_FIRST = {b: [s for s in BESIDE[b] if s[0] in ("onehot", "new")] for b in BESIDE}
    LAST = [("old", 0), ("old", 1), ("old", 2), ("old", 3), ("layer1", 0), ("layer1", 1),
            ("layer1", 2), ("layer1", 3), ("layer2", 0), ("layer3", 0)]
    assert NB == len(BESIDE) and NO == 4

    def acc_use(g, kind, i):
        own = {"onehot": 0, "layer1": NO, "layer2": NO + 2, "layer3": NO + 3}[kind]
        i = i // 2 if kind == "layer1" else i
        if isinstance(g, int) and g == 0:
            return own + i
        if isinstance(g, int) and g == GROUPS:
            return g * (NO + 4) + (own + i - 4) - NO
        return g * (NO + 4) + (own + i - 4)

    def acc_bank(kind, i):
        return acc_use(0, kind, i) % 2

    with ExitStack() as ctx:
        def sb(name, shape, dt=F32):
            return ctx.enter_context(nc.sbuf_tensor(name, shape, dt))

        def psum(name, shape):
            return ctx.enter_context(nc.psum_tensor(name, shape, F32))

        def sem(name):
            return ctx.enter_context(nc.semaphore(name))

        idx = sb("idx", [P, 2, NF], I32)
        rows = sb("rows", [P, 2, NX, D])
        feats = sb("feats", [P, 2, RUNS, QUAD, BLOCK])
        onehot_idx = sb("onehot_idx", [P, len(onehot_f), GROUP], I32)
        row_number = sb("row_number", [P, RC])
        row_number_i = sb("row_number_i", [P, RC], I32)
        onehot = sb("onehot", [P, 2, RC // 2, GROUP], F32R)
        table_high = sb("table_high", [P, len(onehot_f), RC, D], F32R)
        table_low = sb("table_low", [P, len(onehot_f), RC, D], F32R)
        w1_high = sb("w1_high", [P, KC, H1], F32R)
        w1_low = sb("w1_low", [P, KC, H1], F32R)
        w2_high = sb("w2_high", [P, M1, H2], F32R)
        w2_low = sb("w2_low", [P, M1, H2], F32R)
        w3_sb = sb("w3_sb", [P, M2])
        b1_sb = sb("b1_sb", [P, M1])
        b2_sb = sb("b2_sb", [P, M2])
        pairs = sb("pairs", [P, PC, GROUP])
        z_high = sb("z_high", [P, KC, GROUP], F32R)
        z_low = sb("z_low", [P, KC, GROUP], F32R)
        h1 = sb("h1", [P, M1, GROUP])
        h1_high = sb("h1_high", [P, M1, GROUP], F32R)
        h1_low = sb("h1_low", [P, M1, GROUP], F32R)
        h2 = sb("h2", [P, M2, GROUP])
        y_sb = sb("y_sb", [1, GROUP])
        ident = sb("ident", [P, P])
        stage = sb("stage", [P, RC * D])
        STAGE = [stage[:, :], h1[:, :, :].rearrange("p m n -> p (m n)")]

        turned = psum("turned", [P, 2, BANK])
        gram = psum("gram", [P, 2, 2, BANK])
        acc = psum("acc", [P, 2, BANK])

        idx_in = [sem(f"idx_in{t}") for t in range(2)]
        dense_in = [sem(f"dense_in{t}") for t in range(2)]
        gathered = [[sem(f"gathered{t}_{q}") for q in range(NT)] for t in range(2)]
        onehot_idx_in = sem("onehot_idx_in")
        small_in = sem("small_in")
        stage_in = [sem(f"stage_in{k}") for k in range(2)]
        stage_added = sem("stage_added")
        stage_high = sem("stage_high")
        stage_low = sem("stage_low")
        ident_zero = sem("ident_zero")
        ident_ready = sem("ident_ready")
        numbers_made = sem("numbers_made")
        numbers_ready = sem("numbers_ready")
        cleared = sem("cleared")
        turned_ready = sem("turned_ready")
        turned_out = sem("turned_out")
        onehot_ready = sem("onehot_ready")
        onehot_used = sem("onehot_used")
        acc_ready = sem("acc_ready")
        acc_out = sem("acc_out")
        gram_ready = sem("gram_ready")
        gram_out_even = sem("gram_out_even")
        gram_out_odd = sem("gram_out_odd")
        z_high_ready = sem("z_high_ready")
        z_ready = sem("z_ready")
        h1_ready = sem("h1_ready")
        y_stored = sem("y_stored")
        pool_passed = sem("pool_passed")
        sp_passed = sem("sp_passed")

        pieces = []
        for n, f in enumerate(onehot_f):
            pieces.append((tables[f].rearrange("(p c) d -> p c d", c=RC), RP,
                           table_high[0:RP, n, :, :], table_low[0:RP, n, :, :], False))
        for c in range(0, PC, 2):
            e = min(c + 2, PC)
            pieces.append((w1[c:e].rearrange("c p n -> p c n"), P, w1_high[:, c:e, :], w1_low[:, c:e, :], False))
        pieces.append((w1[PC:PC + 2].rearrange("c p n -> p c n"), P, w1_high[:, PC, :], w1_low[:, PC, :], True))
        pieces.append((w2.rearrange("(c p) n -> p c n", p=P), P, w2_high[:, :, :], w2_low[:, :, :], False))
        ADDED = len(pieces) - 2
        PIECES_AT = {b: [n for n in range(2 * b, 2 * b + 2) if n < len(pieces)] for b in range(NB)}

        def staged(n, high):
            a, b = high.shape[1], high.shape[2] if len(high.shape) > 2 else None
            flat = STAGE[n % 2][0:high.shape[0], :]
            if b is None:
                return flat[:, 0:a]
            return flat[:, 0:a * b].rearrange("p (a b) -> p a b", b=b)

        def slot_columns(t, first, count):
            whole = feats[:, t, :, :, :].rearrange("p i s x -> p x s i")
            return whole[:, first:first + count, :, :]

        def by_run(v):
            return v.rearrange("p x (s i) -> p x s i", i=RUNS)

        def gram_block(k, s, j):
            n = len(range(j, NG, QUAD))
            v = gram[BLOCK * s:BLOCK * (s + 1), k, :, 0:(IP // 2) * QUAD * NG]
            v = v.rearrange("p a (i x) -> p a i x", x=QUAD * NG)
            return v[:, :, :, s * NG + j:s * NG + j + QUAD * (n - 1) + 1:QUAD], n

        def pair_block(t, part, s, j, n):
            first = t * P + s * RUNS + part * IP
            v = pairs[BLOCK * j:BLOCK * (j + 1), 0:n, first:first + IP]
            return v.rearrange("p c (a i) -> p a i c", a=2)

        block = ctx.enter_context(nc.Block())

        @block.sync
        def _(sp):
            def load_piece(n):
                if n >= 2:
                    sp.wait_ge(stage_low, n - 1)
                src, p, high, _, two = pieces[n]
                k = src.shape[1] * src.shape[2]
                dst = STAGE[n % 2][0:p, 0:k].rearrange("p (a b) -> p a b", b=src.shape[2])
                sp.dma_start(dst, src).then_inc(stage_in[n % 2], 16)

            def load_tile(g, t):
                at = g * GROUP + t * P
                if not (isinstance(g, int) and g == 0):
                    at = sp.snap(at)
                    for q in range(NT):
                        n = len([x for x in BATCHES[q] if x])
                        sp.wait_ge(gathered[t][q], g * (16 * n))
                        sp.sem_inc(sp_passed, 1)
                sp.dma_start(idx[:, t, :], ids[bass.ds(at, P), :]).then_inc(idx_in[t], 16)
                if not (isinstance(g, int) and g == 0):
                    sp.wait_ge(turned_ready, g * NB + (t * NT + 1 - NB))
                    sp.sem_inc(sp_passed, 1)
                sp.dma_start(rows[:, t, 0, :], dense[bass.ds(at, P), :]).then_inc(dense_in[t], 16)

            def load_onehot_idx(g):
                at = g * GROUP
                if not (isinstance(g, int) and g == 0):
                    at = sp.snap(at)
                    sp.wait_ge(onehot_ready, g * HALVES)
                    sp.sem_inc(sp_passed, 1)
                src = onehot_ids[:, bass.ds(at, GROUP)].rearrange("(o k) b -> o k b", o=1)
                sp.dma_start(onehot_idx[:, :, :], src.to_broadcast([P, len(onehot_f), GROUP]))\
                  .then_inc(onehot_idx_in, 16)

            def store_y(g):
                at = (g - 1) * GROUP if isinstance(g, int) else sp.snap((g - 1) * GROUP)
                sp.wait_ge(acc_out, acc_use(g, "layer3", 0) + 1)
                sp.sem_inc(sp_passed, 1)
                sp.dma_start(y_out[bass.ds(at, GROUP), :].rearrange("b o -> o b"), y_sb[:, :])\
                  .then_inc(y_stored, 16)

            load_tile(0, 0)
            load_tile(0, 1)
            load_onehot_idx(0)
            for n in range(2):
                load_piece(n)
            sp.dma_start(b1_sb[:, :], b1).then_inc(small_in, 16)
            sp.dma_start(b2_sb[:, :], b2).then_inc(small_in, 16)
            sp.dma_start(w3_sb[:, :], w3).then_inc(small_in, 16)
            for n in range(2, len(pieces)):
                load_piece(n)
            with sp.Fori(1, GROUPS) as g:
                load_tile(g, 0)
                load_onehot_idx(g)
                load_tile(g, 1)
                store_y(g)
            store_y(GROUPS)
            sp.wait_ge(y_stored, 16 * GROUPS)

        @block.gpsimd
        def _(pool):
            pool.memset(ident[:, :], 0.0).then_inc(ident_zero, 1)
            pool.iota(row_number_i[:, :], pattern=[[1, RC]], base=0, channel_multiplier=RC)\
                .then_inc(numbers_made, 1)
            pool.wait_ge(ident_zero, 1)
            pool.affine_select(out=ident[:, :], in_=ident[:, :], compare_op=ALU.not_equal, fill=1.0,
                               base=0, pattern=[[-1, P]], channel_multiplier=1).then_inc(ident_ready, 1)

            def gather_group(g, first):
                for t in range(2):
                    pool.wait_ge(idx_in[t], g * 16 + 16)
                    for q in range(NT):
                        if not first:
                            pool.wait_ge(turned_ready, g * NB + (t * NT + q + 1 - NB))
                            pool.sem_inc(pool_passed, 1)
                        for x in BATCHES[q]:
                            if x == 0:
                                continue
                            f = gathered_f[x - 1]
                            pool.indirect_dma_start(
                                out=rows[:, t, x, :], out_offset=None, in_=tables[f],
                                in_offset=bass.IndirectOffsetOnAxis(ap=idx[:, t, f:f + 1], axis=0),
                            ).then_inc(gathered[t][q], 16)

            gather_group(0, True)
            with pool.Fori(1, GROUPS) as g:
                gather_group(g, False)

        @block.tensor
        def _(pe):
            def transposes(g, b, first):
                t, q = divmod(b, NT)
                n = len([x for x in BATCHES[q] if x])
                if q == 0:
                    pe.wait_ge(dense_in[t], g * 16 + 16)
                pe.wait_ge(gathered[t][q], g * (16 * n) + 16 * n)
                if not (first and b < 2):
                    pe.wait_ge(turned_out, g * NB + (b - 1))
                for k, x in enumerate(BATCHES[q]):
                    last = pe.transpose(turned[:, b % 2, k * P:(k + 1) * P], rows[:, t, x, :], ident[:, :])
                last.then_inc(turned_ready, 1)

            def acc_free(g, kind, i, first):
                use = acc_use(g, kind, i)
                if not (first and use < 2):
                    pe.wait_ge(acc_out, use - 1)

            def onehot_bank(g, i, first):
                acc_free(g, "onehot", i, first)
                for n in range(2 * i, min(2 * i + 2, len(onehot_f))):
                    out = acc[:, acc_bank("onehot", i), (n % 2) * GROUP:(n % 2 + 1) * GROUP]
                    if first:
                        pe.wait_ge(stage_low, n + 1)
                    for h in range(2):
                        pe.wait_ge(onehot_ready, g * HALVES + (2 * n + h + 1))
                        for c in range(RC // 2):
                            for part, table in enumerate((table_high, table_low)):
                                last = pe.matmul(out, lhsT=table[0:RP, n, h * (RC // 2) + c, :],
                                                 rhs=onehot[0:RP, h, c, :],
                                                 start=(h == 0 and c == 0 and part == 0),
                                                 stop=(h == 1 and c == RC // 2 - 1 and part == 1))
                        last.then_inc(onehot_used, 1)

            def gram_part(g, t, part, first):
                tile_parts = g * (2 * PARTS) + (t * PARTS + part)
                if part == 0:
                    pe.wait_ge(turned_out, g * NB + (t + 1) * NT)
                    if t == 0:
                        pe.wait_ge(acc_out, acc_use(g, "onehot", NO - 1) + 1)
                k = part % 2
                if not (first and t == 0 and part < 2):
                    done = g * PARTS + (t * (PARTS // 2) + part // 2)
                    pe.wait_ge(gram_out_odd if k else gram_out_even, done)
                for i in range(IP):
                    a, b = divmod(i, IP // 2)
                    last = pe.matmul(gram[:, k, a, b * QUAD * NG:(b + 1) * QUAD * NG],
                                     lhsT=feats[:, t, part * IP + i, :, :].rearrange("p s x -> p (s x)"),
                                     rhs=feats[:, t, part * IP + i, :, 1:SLOTS], start=True, stop=True)
                last.then_inc(gram_ready, 1)

            def passes(out, lhs, rhs, chunks, m):
                (lh, ll), (rh, rl) = lhs, rhs
                todo = [(a, b, c) for c in range(chunks) for a, b in ((lh, rh), (lh, rl), (ll, rh))]
                for n, (a, b, c) in enumerate(todo):
                    last = pe.matmul(out, lhsT=a[:, c, m * P:(m + 1) * P], rhs=b[:, c, :],
                                     start=(n == 0), stop=(n == len(todo) - 1))
                return last

            def layer1(g, m):
                if m == 0:
                    pe.wait_ge(z_ready, g * 2)
                if m % 2 == 0:
                    acc_free(g, "layer1", m, False)
                out = acc[:, acc_bank("layer1", m), (m % 2) * GROUP:(m % 2 + 1) * GROUP]
                last = passes(out, (w1_high, w1_low), (z_high, z_low), KC, m)
                if m % 2:
                    last.then_inc(acc_ready, 1)

            def layer2(g):
                pe.wait_ge(h1_ready, g * 2)
                acc_free(g, "layer2", 0, False)
                for m in range(M2):
                    out = acc[:, acc_bank("layer2", 0), m * GROUP:(m + 1) * GROUP]
                    last = passes(out, (w2_high, w2_low), (h1_high, h1_low), M1, m)
                last.then_inc(acc_ready, 1)

            def layer3(g):
                pe.wait_ge(acc_out, acc_use(g, "layer2", 0) + 1)
                for c in range(M2):
                    last = pe.matmul(acc[0:1, acc_bank("layer3", 0), 0:GROUP], lhsT=w3_sb[:, c:c + 1],
                                     rhs=h2[:, c, :], start=(c == 0), stop=(c == M2 - 1))
                last.then_inc(acc_ready, 1)

            def step(g, what, first=False):
                kind, i = what
                if kind == "old":
                    gram_part(g - 1, 1, i, False)
                elif kind == "new":
                    gram_part(g, 0, i, first)
                elif kind == "onehot":
                    onehot_bank(g, i, first)
                elif kind == "layer1":
                    layer1(g, i)
                elif kind == "layer2":
                    layer2(g)
                else:
                    layer3(g)

            pe.wait_ge(ident_ready, 1)
            pe.wait_ge(cleared, 1)
            for b in range(NB):
                transposes(0, b, True)
                for what in BESIDE_FIRST[b]:
                    step(0, what, True)
            pe.wait_ge(stage_low, len(pieces))
            pe.wait_ge(small_in, 48)
            with pe.Fori(1, GROUPS) as g:
                for b in range(NB):
                    transposes(g, b, False)
                    for what in BESIDE[b]:
                        step(g, what)
            for what in LAST:
                step(GROUPS, what)

        @block.scalar
        def _(act):
            def piece_high(n):
                _, _, high, _, added = pieces[n]
                if added:
                    act.wait_ge(stage_added, 1)
                else:
                    act.wait_ge(stage_in[n % 2], 16 * (n // 2 + 1))
                act.copy(high, staged(n, high)).then_inc(stage_high, 1)

            def turned_move(g, b, first):
                t, q = divmod(b, NT)
                act.wait_ge(turned_ready, g * NB + (b + 1))
                if not first:
                    if q == 0:
                        act.wait_ge(gram_ready, g * (2 * PARTS) + (t - 1) * PARTS)
                        act.wait_ge(z_ready, g * 2 + (t - 1))
                xs = BATCHES[q]
                act.copy(slot_columns(t, xs[0], len(xs)),
                         by_run(turned[:, b % 2, 0:len(xs) * P].rearrange("p (x b) -> p x b", b=P)))\
                   .then_inc(turned_out, 1)

            def onehot_move(g, i, first):
                ns = range(2 * i, min(2 * i + 2, len(onehot_f)))
                act.wait_ge(onehot_used, g * HALVES + (2 * ns[-1] + 2))
                if not first and i == 0:
                    act.wait_ge(gram_ready, g * (2 * PARTS))
                src = acc[:, acc_bank("onehot", i), 0:len(ns) * GROUP].rearrange("p (n b) -> p n b", n=len(ns))
                for t in range(2):
                    last = act.copy(slot_columns(t, NX + ns[0], len(ns)), by_run(src[:, :, t * P:(t + 1) * P]))
                last.then_inc(acc_out, 1)

            def gram_move(g, t, part, first):
                act.wait_ge(gram_ready, g * (2 * PARTS) + (t * PARTS + part + 1))
                if not first and part == 0:
                    act.wait_ge(z_ready, g * 2 + (t - 1))
                for s in range(QUAD):
                    for j in range(QUAD):
                        src, n = gram_block(0, s, j)
                        last = act.copy(pair_block(t, part, s, j, n), src)
                last.then_inc(gram_out_even, 1)

            def split_high(g, t, first):
                act.wait_ge(gram_out_even, g * PARTS + (t + 1) * (PARTS // 2))
                act.wait_ge(gram_out_odd, g * PARTS + (t + 1) * (PARTS // 2))
                if not first:
                    act.wait_ge(acc_ready, layer1_done(g))
                mine = slice(t * P, (t + 1) * P)
                act.copy(z_high[:, 0:PC, mine], pairs[:, :, mine])
                act.copy(by_run(z_high[:, PC:KC, mine]), slot_columns(t, 0, 1)).then_inc(z_high_ready, 1)

            def layer1_done(g):
                return g * 4 - 2

            def relu1(g, half):
                act.wait_ge(acc_ready, g * 4 + (half - 3))
                for m in (2 * half, 2 * half + 1):
                    src = acc[:, acc_bank("layer1", m), (m % 2) * GROUP:(m % 2 + 1) * GROUP]
                    act.activation(h1[:, m, :], src, ACT.Relu, bias=b1_sb[:, m:m + 1])
                    last = act.activation(h1_high[:, m, :], src, ACT.Relu, bias=b1_sb[:, m:m + 1])
                last.then_inc(acc_out, 1)

            def relu2(g):
                act.wait_ge(acc_ready, g * 4 - 1)
                for m in range(M2):
                    last = act.activation(h2[:, m, :], acc[:, acc_bank("layer2", 0), m * GROUP:(m + 1) * GROUP],
                                          ACT.Relu, bias=b2_sb[:, m:m + 1])
                last.then_inc(acc_out, 1)

            def y_move(g, first):
                act.wait_ge(acc_ready, g * 4)
                if not first:
                    act.wait_ge(y_stored, g * 16 - 16)
                act.copy(y_sb[:, :], acc[0:1, acc_bank("layer3", 0), 0:GROUP]).then_inc(acc_out, 1)

            def step(g, what, first=False):
                kind, i = what
                if kind == "old" and i % 2 == 0:
                    gram_move(g - 1, 1, i, g_is(g, 1))
                elif kind == "new" and i % 2 == 0:
                    gram_move(g, 0, i, first)
                elif kind == "onehot":
                    onehot_move(g, i, first)
                elif kind == "layer1" and i % 2:
                    relu1(g, i // 2)
                elif kind == "layer2":
                    relu2(g)
                elif kind == "layer3":
                    y_move(g, g_is(g, 1))

            def g_is(g, n):
                return isinstance(g, int) and g == n

            for b in range(NB):
                for n in PIECES_AT[b]:
                    piece_high(n)
                turned_move(0, b, True)
                for what in BESIDE_FIRST[b]:
                    step(0, what, True)
            act.wait_ge(cleared, 2)
            split_high(0, 0, True)
            act.wait_ge(small_in, 48)

            def group(g):
                for b in range(NB):
                    turned_move(g, b, False)
                    for what in BESIDE[b]:
                        step(g, what)
                    if b == 2:
                        split_high(g - 1, 1, g_is(g, 1))
                    if b == NB - 1:
                        split_high(g, 0, False)

            group(1)
            with act.Fori(2, GROUPS) as g:
                group(g)
            for what in LAST:
                if what == ("layer1", 0):
                    split_high(GROUPS - 1, 1, False)
                step(GROUPS, what)

        @block.vector
        def _(dve):
            dve.memset(feats[:, :, :, :, SLOTS:BLOCK], 0.0).then_inc(cleared, 1)
            dve.memset(pairs[:, :, :], 0.0).then_inc(cleared, 1)
            dve.wait_ge(numbers_made, 1)
            dve.tensor_copy(row_number[:, :], row_number_i[:, :]).then_inc(numbers_ready, 1)
            dve.wait_ge(numbers_ready, 1)
            dve.wait_ge(cleared, 2)

            def piece_low(n):
                src, _, high, low, added = pieces[n]
                if added:
                    dve.wait_ge(stage_in[n % 2], 16 * (n // 2 + 1))
                    both = STAGE[n % 2][:, 0:2 * H1]
                    dve.tensor_add(both[:, 0:H1], both[:, 0:H1], both[:, H1:2 * H1]).then_inc(stage_added, 1)
                dve.wait_ge(stage_high, n + 1)
                dve.tensor_sub(low, staged(n, high), high).then_inc(stage_low, 1)

            def half_table(g, n, first):
                if n == 0:
                    dve.wait_ge(onehot_idx_in, g * 16 + 16)
                if not (first and n < 2):
                    dve.wait_ge(onehot_used, g * HALVES + (n - 1))
                for c in range(RC // 2):
                    k = (n % 2) * (RC // 2) + c
                    last = dve.tensor_scalar(onehot[:, n % 2, c, :], onehot_idx[:, n // 2, :],
                                             row_number[:, k:k + 1], None, ALU.is_equal)
                last.then_inc(onehot_ready, 1)

            def gram_move(g, t, part, first):
                dve.wait_ge(gram_ready, g * (2 * PARTS) + (t * PARTS + part + 1))
                if not first and part == 1:
                    dve.wait_ge(z_ready, g * 2 + (t - 1))
                for s in range(QUAD):
                    for j in range(QUAD):
                        src, n = gram_block(1, s, j)
                        last = dve.tensor_copy(pair_block(t, part, s, j, n), src)
                last.then_inc(gram_out_odd, 1)

            def split_low(g, t):
                dve.wait_ge(z_high_ready, g * 2 + (t + 1))
                mine = slice(t * P, (t + 1) * P)
                dve.tensor_sub(z_low[:, 0:PC, mine], pairs[:, :, mine], z_high[:, 0:PC, mine])
                dve.tensor_sub(by_run(z_low[:, PC:KC, mine]), slot_columns(t, 0, 1), by_run(z_high[:, PC:KC, mine]))\
                   .then_inc(z_ready, 1)

            def h1_split(g, half):
                dve.wait_ge(acc_out, acc_use(g, "layer1", 2 * half) + 1)
                two = slice(2 * half, 2 * half + 2)
                dve.tensor_sub(h1_low[:, two, :], h1[:, two, :], h1_high[:, two, :]).then_inc(h1_ready, 1)

            for b in range(NB):
                for n in PIECES_AT[b]:
                    piece_low(n)
                for kind, i in BESIDE_FIRST[b]:
                    if kind == "onehot":
                        for n in range(4 * i, min(4 * i + 4, HALVES)):
                            half_table(0, n, True)
                    if kind == "new" and i % 2:
                        gram_move(0, 0, i, True)
            split_low(0, 0)

            def group(g, second):
                half_table(g, 0, False)
                half_table(g, 1, False)
                gram_move(g - 1, 1, 1, second)
                half_table(g, 2, False)
                gram_move(g - 1, 1, 3, second)
                half_table(g, 3, False)
                split_low(g - 1, 1)
                for n in range(4, HALVES):
                    half_table(g, n, False)
                h1_split(g, 0)
                gram_move(g, 0, 1, False)
                h1_split(g, 1)
                gram_move(g, 0, 3, False)
                split_low(g, 0)

            group(1, True)
            with dve.Fori(2, GROUPS) as g:
                group(g, False)
            gram_move(GROUPS - 1, 1, 1, False)
            gram_move(GROUPS - 1, 1, 3, False)
            split_low(GROUPS - 1, 1)
            h1_split(GROUPS, 0)
            h1_split(GROUPS, 1)


def kernel(**inputs):
    import concourse.bacc as bacc
    from concourse.bass_utils import run_bass_kernel_spmd

    tables = [np.ascontiguousarray(inputs[f"tbl_{f}"]) for f in range(26)]
    gathered_f, onehot_f = feature_order([t.shape[0] for t in tables])
    slots = len(tables) + 1
    feature = [0] + [f + 1 for f in gathered_f + onehot_f]

    w1 = np.asarray(inputs["W_top1"])
    number = np.full((slots, slots), -1)
    number[np.triu_indices(slots, 1)] = np.arange(slots * (slots - 1) // 2)
    chunks = pair_chunks(slots)
    laid = np.zeros((chunks + 2, P, w1.shape[1]), w1.dtype)
    for g in range(1, slots):
        c, j = divmod(g - 1, QUAD)
        for f in range(g):
            a, b = sorted((feature[f], feature[g]))
            laid[c, BLOCK * j + f] = w1[D + number[a, b]]
    laid[chunks] = w1[0:D]
    laid[chunks + 1] = w1[w1.shape[0] - D:]

    ids = np.ascontiguousarray(inputs["ids"])
    arrays = {
        "dense": np.ascontiguousarray(inputs["r_dense_features"]),
        "ids": ids,
        "onehot_ids": np.ascontiguousarray(ids.T[onehot_f]),
        "w1": laid,
        "b1": np.ascontiguousarray(np.asarray(inputs["b_top1"]).reshape(-1, P).T),
        "w2": np.ascontiguousarray(inputs["W_top2"]),
        "b2": np.ascontiguousarray(np.asarray(inputs["b_top2"]).reshape(-1, P).T),
        "w3": np.ascontiguousarray(np.asarray(inputs["W_top3"]).reshape(-1, P).T),
    }
    for f, t in enumerate(tables):
        arrays[f"tbl_{f}"] = t

    nc = bacc.Bacc("TRN2", target_bir_lowering=False, num_devices=1)
    aps = {n: nc.dram_tensor(n, a.shape, mybir.dt.from_np(a.dtype), kind="ExternalInput").ap()
           for n, a in arrays.items()}
    y = nc.dram_tensor("y", (ids.shape[0], 1), F32, kind="ExternalOutput").ap()
    build_tower(nc, aps["dense"], aps["ids"], aps["onehot_ids"], [aps[f"tbl_{f}"] for f in range(26)],
                aps["w1"], aps["b1"], aps["w2"], aps["b2"], aps["w3"], y)
    result = run_bass_kernel_spmd(nc, [arrays], core_ids=[0])
    return result.results[0]["y"]
```

```python
from contextlib import ExitStack

import numpy as np

import concourse.bass as bass
from concourse import mybir

F32 = mybir.dt.float32
F32R = mybir.dt.float32r
I32 = mybir.dt.int32
ALU = mybir.AluOpType
ACT = mybir.ActivationFunctionType

P = 128
D = 128
GROUP = 2 * P
ONEHOT = 6
QUAD = 4
BLOCK = 32
BANK = 512


def feature_order(rows):
    small = sorted(sorted(range(len(rows)), key=lambda f: (rows[f], f))[:ONEHOT])
    return [f for f in range(len(rows)) if f not in small], small


def pair_chunks(slots):
    return -(-(slots - 1) // QUAD)


def build_tower(nc, dense, ids, onehot_ids, tables, w1, b1, w2, b2, w3, y_out):
    SAMPLES = dense.shape[0]
    GROUPS = SAMPLES // GROUP
    NF = len(tables)
    SLOTS = NF + 1
    gathered_f, onehot_f = feature_order([t.shape[0] for t in tables])
    NX = 1 + len(gathered_f)
    PER = BANK // P
    NT = -(-NX // PER)
    BATCHES = [list(range(-(-NX * q // NT), -(-NX * (q + 1) // NT))) for q in range(NT)]
    NB = 2 * NT
    TABLE_ROWS = tables[onehot_f[0]].shape[0]
    assert all(tables[f].shape[0] == TABLE_ROWS for f in onehot_f)
    RC = 8
    RP = TABLE_ROWS // RC
    assert RP * RC == TABLE_ROWS and RP <= P
    HALVES = 2 * len(onehot_f)
    NO = -(-len(onehot_f) // 2)
    PC = pair_chunks(SLOTS)
    KC = PC + 1
    H1, H2 = w1.shape[2], w2.shape[1]
    M1, M2 = H1 // P, H2 // P
    NG = SLOTS - 1
    NF_ROWS = SLOTS - 1
    RUNS = P // QUAD
    LHS = BLOCK * (QUAD - 1) + NF_ROWS
    PARTS = 4
    IP = RUNS // PARTS
    assert M1 == 4 and IP * QUAD * NG <= 2 * BANK and BLOCK * QUAD == P

    BESIDE = {
        0: [("old", 0), ("old", 1)],
        1: [("old", 2), ("old", 3)],
        2: [("onehot", 0)],
        3: [("onehot", 1)],
        4: [("layer1", 0)],
        5: [("layer1", 1)],
        6: [("onehot", 2)],
        7: [("layer1", 2)],
        8: [("layer1", 3)],
        9: [("new", 0), ("new", 1)],
        10: [("new", 2), ("new", 3), ("layer2", 0)],
        11: [("layer3", 0)],
    }
    BESIDE_FIRST = {b: [s for s in BESIDE[b] if s[0] in ("onehot", "new")] for b in BESIDE}
    LAST = [("old", 0), ("old", 1), ("old", 2), ("old", 3), ("layer1", 0), ("layer1", 1),
            ("layer1", 2), ("layer1", 3), ("layer2", 0), ("layer3", 0)]
    assert NB == len(BESIDE) and NO == 3

    def uses(steps):
        return [(kind, i // 2 if kind == "layer1" else i) for kind, i in steps
                if kind in ("onehot", "layer2", "layer3") or (kind == "layer1" and i % 2)]

    USES_FIRST = uses([s for b in BESIDE for s in BESIDE_FIRST[b]])
    USES = uses([s for b in BESIDE for s in BESIDE[b]])
    USES_LAST = uses(LAST)
    assert len(USES_FIRST) % 2 == len(USES) % 2

    def acc_use(g, kind, i):
        which = (kind, i // 2 if kind == "layer1" else i)
        if isinstance(g, int) and g == 0:
            return USES_FIRST.index(which)
        order = USES_LAST if isinstance(g, int) and g == GROUPS else USES
        return g * len(USES) + (order.index(which) - len(USES) + len(USES_FIRST))

    def acc_place(g, kind, i):
        order = USES
        if isinstance(g, int) and g in (0, GROUPS):
            order = USES_FIRST if g == 0 else USES_LAST
        return order.index((kind, i // 2 if kind == "layer1" else i))

    def acc_bank(g, kind, i):
        return acc_place(g, kind, i) % 2

    def acc_distance(g, kind, i):
        place = acc_place(g, kind, i)
        return 2 if place >= 2 or len(USES) % 2 == 0 else 1 + 2 * place

    with ExitStack() as ctx:
        def sb(name, shape, dt=F32):
            return ctx.enter_context(nc.sbuf_tensor(name, shape, dt))

        def psum(name, shape):
            return ctx.enter_context(nc.psum_tensor(name, shape, F32))

        def sem(name):
            return ctx.enter_context(nc.semaphore(name))

        idx = sb("idx", [P, 2, NF], I32)
        rows = sb("rows", [P, 2, NX, D])
        feats = sb("feats", [P, 2, RUNS, QUAD, BLOCK])
        onehot_idx = sb("onehot_idx", [P, len(onehot_f), GROUP], I32)
        first_row = sb("first_row", [P, 1])
        first_row_i = sb("first_row_i", [P, 1], I32)
        onehot = sb("onehot", [P, 2, RC // 2, GROUP], F32R)
        table_high = sb("table_high", [P, len(onehot_f), RC, D], F32R)
        table_low = sb("table_low", [P, len(onehot_f), RC, D], F32R)
        w1_high = sb("w1_high", [P, KC, H1], F32R)
        w1_low = sb("w1_low", [P, KC, H1], F32R)
        w2_high = sb("w2_high", [P, M1, H2], F32R)
        w2_low = sb("w2_low", [P, M1, H2], F32R)
        w3_sb = sb("w3_sb", [P, M2])
        b1_sb = sb("b1_sb", [P, M1])
        b2_sb = sb("b2_sb", [P, M2])
        pairs = sb("pairs", [P, PC, GROUP])
        z_high = sb("z_high", [P, KC, GROUP], F32R)
        z_low = sb("z_low", [P, KC, GROUP], F32R)
        h1 = sb("h1", [P, M1, GROUP])
        h1_high = sb("h1_high", [P, M1, GROUP], F32R)
        h1_low = sb("h1_low", [P, M1, GROUP], F32R)
        h2 = sb("h2", [P, M2, GROUP])
        y_sb = sb("y_sb", [1, GROUP])
        ident = sb("ident", [P, P])
        stage = sb("stage", [P, RC * D])
        STAGE = [stage[:, :], h1[:, :, :].rearrange("p m n -> p (m n)")]

        turned = psum("turned", [P, 2, BANK])
        gram = psum("gram", [P, 2, 2, BANK])
        acc = psum("acc", [P, 2, BANK])

        idx_in = [sem(f"idx_in{t}") for t in range(2)]
        dense_in = [sem(f"dense_in{t}") for t in range(2)]
        gathered = [[sem(f"gathered{t}_{q}") for q in range(NT)] for t in range(2)]
        onehot_idx_in = sem("onehot_idx_in")
        small_in = sem("small_in")
        stage_in = [sem(f"stage_in{k}") for k in range(2)]
        stage_added = sem("stage_added")
        stage_high = sem("stage_high")
        stage_low = sem("stage_low")
        ident_zero = sem("ident_zero")
        ident_ready = sem("ident_ready")
        numbers_made = sem("numbers_made")
        numbers_ready = sem("numbers_ready")
        cleared = sem("cleared")
        turned_ready = sem("turned_ready")
        turned_out = sem("turned_out")
        onehot_ready = sem("onehot_ready")
        onehot_used = sem("onehot_used")
        acc_ready = sem("acc_ready")
        acc_out = sem("acc_out")
        gram_ready = sem("gram_ready")
        gram_out_even = sem("gram_out_even")
        gram_out_odd = sem("gram_out_odd")
        idx_relative = sem("idx_relative")
        dense_high_ready = sem("dense_high_ready")
        dense_ready = sem("dense_ready")
        z_high_ready = sem("z_high_ready")
        z_ready = sem("z_ready")
        h1_ready = sem("h1_ready")
        y_stored = sem("y_stored")
        pool_passed = sem("pool_passed")
        sp_passed = sem("sp_passed")
        act_passed = sem("act_passed")

        pieces = []
        for n, f in enumerate(onehot_f):
            pieces.append((tables[f].rearrange("(p c) d -> p c d", c=RC), RP,
                           table_high[0:RP, n, :, :], table_low[0:RP, n, :, :], False))
        for c in range(0, PC, 2):
            e = min(c + 2, PC)
            pieces.append((w1[c:e].rearrange("c p n -> p c n"), P, w1_high[:, c:e, :], w1_low[:, c:e, :], False))
        pieces.append((w1[PC:PC + 2].rearrange("c p n -> p c n"), P, w1_high[:, PC, :], w1_low[:, PC, :], True))
        pieces.append((w2.rearrange("(c p) n -> p c n", p=P), P, w2_high[:, :, :], w2_low[:, :, :], False))
        ADDED = len(pieces) - 2
        PIECES_AT = {b: [] for b in range(NB)}
        PIECES_AT[0] = list(range(len(onehot_f)))
        for n in range(len(onehot_f), len(pieces)):
            PIECES_AT[min(NB - 1, NT + n - len(onehot_f))].append(n)

        def staged(n, high):
            a, b = high.shape[1], high.shape[2] if len(high.shape) > 2 else None
            flat = STAGE[n % 2][0:high.shape[0], :]
            if b is None:
                return flat[:, 0:a]
            return flat[:, 0:a * b].rearrange("p (a b) -> p a b", b=b)

        def slot_columns(t, first, count):
            whole = feats[:, t, :, :, :].rearrange("p i s x -> p x s i")
            return whole[:, first:first + count, :, :]

        def by_run(v):
            return v.rearrange("p x (s i) -> p x s i", i=RUNS)

        def gram_block(k, s, j):
            n = len(range(j, NG, QUAD))
            v = gram[BLOCK * s:BLOCK * s + NF_ROWS, k, :, 0:(IP // 2) * QUAD * NG]
            v = v.rearrange("p a (i x) -> p a i x", x=QUAD * NG)
            return v[:, :, :, s * NG + j:s * NG + j + QUAD * (n - 1) + 1:QUAD], n

        def pair_block(t, part, s, j, n):
            first = t * P + s * RUNS + part * IP
            v = pairs[BLOCK * j:BLOCK * j + NF_ROWS, 0:n, first:first + IP]
            return v.rearrange("p c (a i) -> p a i c", a=2)

        block = ctx.enter_context(nc.Block())

        @block.sync
        def _(sp):
            def load_piece(n):
                if n >= 2:
                    sp.wait_ge(stage_low, n - 1)
                src, p, high, _, two = pieces[n]
                k = src.shape[1] * src.shape[2]
                dst = STAGE[n % 2][0:p, 0:k].rearrange("p (a b) -> p a b", b=src.shape[2])
                sp.dma_start(dst, src).then_inc(stage_in[n % 2], 16)

            def load_tile(g, t):
                at = g * GROUP + t * P
                if not (isinstance(g, int) and g == 0):
                    at = sp.snap(at)
                    for q in range(NT):
                        n = len([x for x in BATCHES[q] if x])
                        sp.wait_ge(gathered[t][q], g * (16 * n))
                        sp.sem_inc(sp_passed, 1)
                sp.dma_start(idx[:, t, :], ids[bass.ds(at, P), :]).then_inc(idx_in[t], 16)
                if not (isinstance(g, int) and g == 0):
                    sp.wait_ge(turned_ready, g * NB + (t * NT + 1 - NB))
                    sp.sem_inc(sp_passed, 1)
                sp.dma_start(rows[:, t, 0, :], dense[bass.ds(at, P), :]).then_inc(dense_in[t], 16)

            def load_onehot_idx(g):
                at = g * GROUP
                if not (isinstance(g, int) and g == 0):
                    at = sp.snap(at)
                    sp.wait_ge(onehot_ready, g * HALVES)
                    sp.sem_inc(sp_passed, 1)
                src = onehot_ids[:, bass.ds(at, GROUP)].rearrange("(o k) b -> o k b", o=1)
                sp.dma_start(onehot_idx[:, :, :], src.to_broadcast([P, len(onehot_f), GROUP]))\
                  .then_inc(onehot_idx_in, 16)

            load_tile(0, 0)
            load_tile(0, 1)
            load_onehot_idx(0)
            for n in range(2):
                load_piece(n)
            sp.dma_start(b1_sb[:, :], b1).then_inc(small_in, 16)
            sp.dma_start(b2_sb[:, :], b2).then_inc(small_in, 16)
            sp.dma_start(w3_sb[:, :], w3).then_inc(small_in, 16)
            for n in range(2, len(pieces)):
                load_piece(n)
            with sp.Fori(1, GROUPS) as g:
                load_tile(g, 0)
                load_onehot_idx(g)
                load_tile(g, 1)

        @block.gpsimd
        def _(pool):
            pool.memset(ident[:, :], 0.0).then_inc(ident_zero, 1)
            pool.iota(first_row_i[:, :], pattern=[[0, 1]], base=0, channel_multiplier=RC)\
                .then_inc(numbers_made, 1)
            pool.wait_ge(ident_zero, 1)
            pool.affine_select(out=ident[:, :], in_=ident[:, :], compare_op=ALU.not_equal, fill=1.0,
                               base=0, pattern=[[-1, P]], channel_multiplier=1).then_inc(ident_ready, 1)

            def gather_group(g, first):
                for t in range(2):
                    pool.wait_ge(idx_in[t], g * 16 + 16)
                    for q in range(NT):
                        if not first:
                            pool.wait_ge(turned_ready, g * NB + (t * NT + q + 1 - NB))
                            pool.sem_inc(pool_passed, 1)
                        for x in BATCHES[q]:
                            if x == 0:
                                continue
                            f = gathered_f[x - 1]
                            pool.indirect_dma_start(
                                out=rows[:, t, x, :], out_offset=None, in_=tables[f],
                                in_offset=bass.IndirectOffsetOnAxis(ap=idx[:, t, f:f + 1], axis=0),
                            ).then_inc(gathered[t][q], 16)

            gather_group(0, True)
            with pool.Fori(1, GROUPS) as g:
                gather_group(g, False)

        @block.tensor
        def _(pe):
            def transposes(g, b, first):
                t, q = divmod(b, NT)
                n = len([x for x in BATCHES[q] if x])
                if q == 0:
                    pe.wait_ge(dense_in[t], g * 16 + 16)
                pe.wait_ge(gathered[t][q], g * (16 * n) + 16 * n)
                if not (first and b < 2):
                    pe.wait_ge(turned_out, g * NB + (b - 1))
                for k, x in enumerate(BATCHES[q]):
                    last = pe.transpose(turned[:, b % 2, k * P:(k + 1) * P], rows[:, t, x, :], ident[:, :])
                last.then_inc(turned_ready, 1)

            def acc_free(g, kind, i, first):
                use = acc_use(g, kind, i)
                if not (first and use < 2):
                    pe.wait_ge(acc_out, use - acc_distance(g, kind, i) + 1)

            def onehot_bank(g, i, first):
                acc_free(g, "onehot", i, first)
                for n in range(2 * i, min(2 * i + 2, len(onehot_f))):
                    out = acc[:, acc_bank(g, "onehot", i), (n % 2) * GROUP:(n % 2 + 1) * GROUP]
                    if first:
                        pe.wait_ge(stage_low, n + 1)
                    for h in range(2):
                        pe.wait_ge(onehot_ready, g * HALVES + (2 * n + h + 1))
                        for c in range(RC // 2):
                            for part, table in enumerate((table_high, table_low)):
                                last = pe.matmul(out, lhsT=table[0:RP, n, h * (RC // 2) + c, :],
                                                 rhs=onehot[0:RP, h, c, :],
                                                 start=(h == 0 and c == 0 and part == 0),
                                                 stop=(h == 1 and c == RC // 2 - 1 and part == 1))
                        last.then_inc(onehot_used, 1)

            def gram_part(g, t, part, first):
                tile_parts = g * (2 * PARTS) + (t * PARTS + part)
                if part == 0:
                    pe.wait_ge(turned_out, g * NB + (t + 1) * NT)
                    if t == 0:
                        pe.wait_ge(acc_out, acc_use(g, "onehot", NO - 1) + 1)
                k = part % 2
                if not (first and t == 0 and part < 2):
                    done = g * PARTS + (t * (PARTS // 2) + part // 2)
                    pe.wait_ge(gram_out_odd if k else gram_out_even, done)
                for i in range(IP):
                    a, b = divmod(i, IP // 2)
                    last = pe.matmul(gram[0:LHS, k, a, b * QUAD * NG:(b + 1) * QUAD * NG],
                                     lhsT=feats[:, t, part * IP + i, :, :].rearrange("p s x -> p (s x)")[:, 0:LHS],
                                     rhs=feats[:, t, part * IP + i, :, 1:SLOTS], start=True, stop=True)
                last.then_inc(gram_ready, 1)

            def passes(out, lhs, rhs, chunks, m):
                (lh, ll), (rh, rl) = lhs, rhs
                todo = [(a, b, c) for c in range(chunks) for a, b in ((lh, rh), (lh, rl), (ll, rh))]
                for n, (a, b, c) in enumerate(todo):
                    last = pe.matmul(out, lhsT=a[:, c, m * P:(m + 1) * P], rhs=b[:, c, :],
                                     start=(n == 0), stop=(n == len(todo) - 1))
                return last

            def layer1(g, m):
                if m == 0:
                    pe.wait_ge(z_ready, g * 2)
                if m % 2 == 0:
                    acc_free(g, "layer1", m, False)
                out = acc[:, acc_bank(g, "layer1", m), (m % 2) * GROUP:(m % 2 + 1) * GROUP]
                last = passes(out, (w1_high, w1_low), (z_high, z_low), KC, m)
                if m % 2:
                    last.then_inc(acc_ready, 1)

            def layer2(g):
                pe.wait_ge(h1_ready, g * 2)
                acc_free(g, "layer2", 0, False)
                for m in range(M2):
                    out = acc[:, acc_bank(g, "layer2", 0), m * GROUP:(m + 1) * GROUP]
                    last = passes(out, (w2_high, w2_low), (h1_high, h1_low), M1, m)
                last.then_inc(acc_ready, 1)

            def layer3(g):
                pe.wait_ge(acc_out, acc_use(g, "layer2", 0) + 1)
                for c in range(M2):
                    last = pe.matmul(acc[0:1, acc_bank(g, "layer3", 0), 0:GROUP], lhsT=w3_sb[:, c:c + 1],
                                     rhs=h2[:, c, :], start=(c == 0), stop=(c == M2 - 1))
                last.then_inc(acc_ready, 1)

            def step(g, what, first=False):
                kind, i = what
                if kind == "old":
                    gram_part(g - 1, 1, i, False)
                elif kind == "new":
                    gram_part(g, 0, i, first)
                elif kind == "onehot":
                    onehot_bank(g, i, first)
                elif kind == "layer1":
                    layer1(g, i)
                elif kind == "layer2":
                    layer2(g)
                else:
                    layer3(g)

            pe.wait_ge(ident_ready, 1)
            pe.wait_ge(cleared, 1)
            for b in range(NB):
                transposes(0, b, True)
                for what in BESIDE_FIRST[b]:
                    step(0, what, True)
            pe.wait_ge(stage_low, len(pieces))
            pe.wait_ge(small_in, 48)
            with pe.Fori(1, GROUPS) as g:
                for b in range(NB):
                    transposes(g, b, False)
                    for what in BESIDE[b]:
                        step(g, what)
            for what in LAST:
                step(GROUPS, what)

        @block.scalar
        def _(act):
            def piece_high(n):
                _, _, high, _, added = pieces[n]
                if added:
                    act.wait_ge(stage_added, 1)
                else:
                    act.wait_ge(stage_in[n % 2], 16 * (n // 2 + 1))
                act.copy(high, staged(n, high)).then_inc(stage_high, 1)

            def turned_move(g, b, first):
                t, q = divmod(b, NT)
                act.wait_ge(turned_ready, g * NB + (b + 1))
                if not first:
                    if q == 0:
                        act.wait_ge(gram_ready, g * (2 * PARTS) + (t - 1) * PARTS)
                        act.wait_ge(dense_ready, g * 2 + (t - 1))
                xs = BATCHES[q]
                act.copy(slot_columns(t, xs[0], len(xs)),
                         by_run(turned[:, b % 2, 0:len(xs) * P].rearrange("p (x b) -> p x b", b=P)))\
                   .then_inc(turned_out, 1)

            def onehot_move(g, i, first):
                ns = range(2 * i, min(2 * i + 2, len(onehot_f)))
                act.wait_ge(onehot_used, g * HALVES + (2 * ns[-1] + 2))
                if not first and i == 0:
                    act.wait_ge(gram_ready, g * (2 * PARTS))
                src = acc[:, acc_bank(g, "onehot", i), 0:len(ns) * GROUP].rearrange("p (n b) -> p n b", n=len(ns))
                for t in range(2):
                    last = act.copy(slot_columns(t, NX + ns[0], len(ns)), by_run(src[:, :, t * P:(t + 1) * P]))
                last.then_inc(acc_out, 1)

            def gram_move(g, t, part, first):
                act.wait_ge(gram_ready, g * (2 * PARTS) + (t * PARTS + part + 1))
                if first and part == 0:
                    act.wait_ge(cleared, 2)
                for s in range(QUAD):
                    for j in range(QUAD):
                        src, n = gram_block(0, s, j)
                        last = act.copy(pair_block(t, part, s, j, n), src)
                last.then_inc(gram_out_even, 1)

            def relu1(g, half):
                act.wait_ge(acc_ready, g * 4 + (half - 3))
                for m in (2 * half, 2 * half + 1):
                    src = acc[:, acc_bank(g, "layer1", m), (m % 2) * GROUP:(m % 2 + 1) * GROUP]
                    act.activation(h1[:, m, :], src, ACT.Relu, bias=b1_sb[:, m:m + 1])
                    last = act.activation(h1_high[:, m, :], src, ACT.Relu, bias=b1_sb[:, m:m + 1])
                last.then_inc(acc_out, 1)

            def relu2(g):
                act.wait_ge(acc_ready, g * 4 - 1)
                for m in range(M2):
                    last = act.activation(h2[:, m, :], acc[:, acc_bank(g, "layer2", 0), m * GROUP:(m + 1) * GROUP],
                                          ACT.Relu, bias=b2_sb[:, m:m + 1])
                last.then_inc(acc_out, 1)

            def y_move(g, first):
                act.wait_ge(acc_ready, g * 4)
                if not first:
                    act.wait_ge(y_stored, g * 16 - 16)
                act.copy(y_sb[:, :], acc[0:1, acc_bank(g, "layer3", 0), 0:GROUP]).then_inc(acc_out, 1)
                at = (g - 1) * GROUP if isinstance(g, int) else act.snap((g - 1) * GROUP)
                act.wait_ge(acc_out, acc_use(g, "layer3", 0) + 1)
                act.sem_inc(act_passed, 1)
                act.dma_start(y_out[bass.ds(at, GROUP), :].rearrange("b o -> o b"), y_sb[:, :])\
                   .then_inc(y_stored, 16)

            def step(g, what, first=False):
                kind, i = what
                if kind == "old" and i % 2 == 0:
                    gram_move(g - 1, 1, i, g_is(g, 1))
                elif kind == "new" and i % 2 == 0:
                    gram_move(g, 0, i, first)
                elif kind == "onehot":
                    onehot_move(g, i, first)
                elif kind == "layer1" and i % 2:
                    relu1(g, i // 2)
                elif kind == "layer2":
                    relu2(g)
                elif kind == "layer3":
                    y_move(g, g_is(g, 1))

            def g_is(g, n):
                return isinstance(g, int) and g == n

            for b in range(NB):
                for n in PIECES_AT[b]:
                    piece_high(n)
                turned_move(0, b, True)
                for what in BESIDE_FIRST[b]:
                    step(0, what, True)
            act.wait_ge(small_in, 48)

            def group(g):
                for b in range(NB):
                    turned_move(g, b, False)
                    for what in BESIDE[b]:
                        step(g, what)

            group(1)
            with act.Fori(2, GROUPS) as g:
                group(g)
            for what in LAST:
                step(GROUPS, what)
            act.wait_ge(y_stored, 16 * GROUPS)

        @block.vector
        def _(dve):
            dve.memset(feats[:, :, :, :, SLOTS:BLOCK], 0.0).then_inc(cleared, 1)
            dve.memset(pairs[:, :, :], 0.0).then_inc(cleared, 1)
            dve.wait_ge(numbers_made, 1)
            dve.tensor_copy(first_row[:, :], first_row_i[:, :]).then_inc(numbers_ready, 1)
            dve.wait_ge(numbers_ready, 1)
            dve.wait_ge(cleared, 2)

            def piece_low(n):
                src, _, high, low, added = pieces[n]
                if added:
                    dve.wait_ge(stage_in[n % 2], 16 * (n // 2 + 1))
                    both = STAGE[n % 2][:, 0:2 * H1]
                    dve.tensor_add(both[:, 0:H1], both[:, 0:H1], both[:, H1:2 * H1]).then_inc(stage_added, 1)
                dve.wait_ge(stage_high, n + 1)
                dve.tensor_sub(low, staged(n, high), high).then_inc(stage_low, 1)

            def half_table(g, n, first):
                if n == 0:
                    dve.wait_ge(onehot_idx_in, g * 16 + 16)
                    dve.tensor_scalar(onehot_idx[:, :, :], onehot_idx[:, :, :], first_row[:, 0:1], None,
                                      ALU.subtract).then_inc(idx_relative, 1)
                    dve.wait_ge(idx_relative, g + 1)
                if not (first and n < 2):
                    dve.wait_ge(onehot_used, g * HALVES + (n - 1))
                for c in range(RC // 2):
                    k = (n % 2) * (RC // 2) + c
                    last = dve.tensor_scalar(onehot[:, n % 2, c, :], onehot_idx[:, n // 2, :],
                                             float(k), None, ALU.is_equal)
                last.then_inc(onehot_ready, 1)

            def gram_move(g, t, part):
                dve.wait_ge(gram_ready, g * (2 * PARTS) + (t * PARTS + part + 1))
                for s in range(QUAD):
                    for j in range(QUAD):
                        src, n = gram_block(1, s, j)
                        last = dve.tensor_copy(pair_block(t, part, s, j, n), src)
                last.then_inc(gram_out_odd, 1)

            def layer1_done(g):
                return g * 4 - 2

            def split_dense(g, t, first):
                dve.wait_ge(turned_out, g * NB + (t * NT + 1))
                if not first:
                    dve.wait_ge(acc_ready, layer1_done(g))
                mine = slice(t * P, (t + 1) * P)
                high, low = by_run(z_high[:, PC:KC, mine]), by_run(z_low[:, PC:KC, mine])
                dve.tensor_copy(high, slot_columns(t, 0, 1)).then_inc(dense_high_ready, 1)
                dve.wait_ge(dense_high_ready, g * 2 + (t + 1))
                dve.tensor_sub(low, slot_columns(t, 0, 1), high).then_inc(dense_ready, 1)

            def split_pairs(g, t):
                dve.wait_ge(gram_out_even, g * PARTS + (t + 1) * (PARTS // 2))
                dve.wait_ge(gram_out_odd, g * PARTS + (t + 1) * (PARTS // 2))
                mine = slice(t * P, (t + 1) * P)
                dve.tensor_copy(z_high[:, 0:PC, mine], pairs[:, :, mine]).then_inc(z_high_ready, 1)
                dve.wait_ge(z_high_ready, g * 2 + (t + 1))
                dve.tensor_sub(z_low[:, 0:PC, mine], pairs[:, :, mine], z_high[:, 0:PC, mine])\
                   .then_inc(z_ready, 1)

            def h1_split(g, half):
                dve.wait_ge(acc_out, acc_use(g, "layer1", 2 * half) + 1)
                two = slice(2 * half, 2 * half + 2)
                dve.tensor_sub(h1_low[:, two, :], h1[:, two, :], h1_high[:, two, :]).then_inc(h1_ready, 1)

            for b in range(NB):
                for n in PIECES_AT[b]:
                    piece_low(n)
                for kind, i in BESIDE_FIRST[b]:
                    if kind == "onehot":
                        for n in range(4 * i, min(4 * i + 4, HALVES)):
                            half_table(0, n, True)
                    if kind == "new" and i % 2:
                        gram_move(0, 0, i)
            split_dense(0, 0, True)
            split_dense(0, 1, True)
            half_table(1, 0, False)
            half_table(1, 1, False)
            split_pairs(0, 0)

            def group(g, last):
                gram_move(g - 1, 1, 1)
                gram_move(g - 1, 1, 3)
                half_table(g, 2, False)
                half_table(g, 3, False)
                split_pairs(g - 1, 1)
                for n in range(4, 10):
                    half_table(g, n, False)
                h1_split(g, 0)
                for n in range(10, HALVES):
                    half_table(g, n, False)
                h1_split(g, 1)
                split_dense(g, 0, False)
                gram_move(g, 0, 1)
                split_dense(g, 1, False)
                if not last:
                    half_table(g + 1, 0, False)
                    half_table(g + 1, 1, False)
                gram_move(g, 0, 3)
                split_pairs(g, 0)

            with dve.Fori(1, GROUPS - 1) as g:
                group(g, False)
            group(GROUPS - 1, True)
            gram_move(GROUPS - 1, 1, 1)
            gram_move(GROUPS - 1, 1, 3)
            split_pairs(GROUPS - 1, 1)
            h1_split(GROUPS, 0)
            h1_split(GROUPS, 1)


def kernel(**inputs):
    import concourse.bacc as bacc
    from concourse.bass_utils import run_bass_kernel_spmd

    tables = [np.ascontiguousarray(inputs[f"tbl_{f}"]) for f in range(26)]
    gathered_f, onehot_f = feature_order([t.shape[0] for t in tables])
    slots = len(tables) + 1
    feature = [0] + [f + 1 for f in gathered_f + onehot_f]

    w1 = np.asarray(inputs["W_top1"])
    number = np.full((slots, slots), -1)
    number[np.triu_indices(slots, 1)] = np.arange(slots * (slots - 1) // 2)
    chunks = pair_chunks(slots)
    laid = np.zeros((chunks + 2, P, w1.shape[1]), w1.dtype)
    for g in range(1, slots):
        c, j = divmod(g - 1, QUAD)
        for f in range(g):
            a, b = sorted((feature[f], feature[g]))
            laid[c, BLOCK * j + f] = w1[D + number[a, b]]
    laid[chunks] = w1[0:D]
    laid[chunks + 1] = w1[w1.shape[0] - D:]

    ids = np.ascontiguousarray(inputs["ids"])
    arrays = {
        "dense": np.ascontiguousarray(inputs["r_dense_features"]),
        "ids": ids,
        "onehot_ids": np.ascontiguousarray(ids.T[onehot_f]),
        "w1": laid,
        "b1": np.ascontiguousarray(np.asarray(inputs["b_top1"]).reshape(-1, P).T),
        "w2": np.ascontiguousarray(inputs["W_top2"]),
        "b2": np.ascontiguousarray(np.asarray(inputs["b_top2"]).reshape(-1, P).T),
        "w3": np.ascontiguousarray(np.asarray(inputs["W_top3"]).reshape(-1, P).T),
    }
    for f, t in enumerate(tables):
        arrays[f"tbl_{f}"] = t

    nc = bacc.Bacc("TRN2", target_bir_lowering=False, num_devices=1)
    aps = {n: nc.dram_tensor(n, a.shape, mybir.dt.from_np(a.dtype), kind="ExternalInput").ap()
           for n, a in arrays.items()}
    y = nc.dram_tensor("y", (ids.shape[0], 1), F32, kind="ExternalOutput").ap()
    build_tower(nc, aps["dense"], aps["ids"], aps["onehot_ids"], [aps[f"tbl_{f}"] for f in range(26)],
                aps["w1"], aps["b1"], aps["w2"], aps["b2"], aps["w3"], y)
    result = run_bass_kernel_spmd(nc, [arrays], core_ids=[0])
    return result.results[0]["y"]
```

```python
from contextlib import ExitStack

import numpy as np

import concourse.bass as bass
from concourse import mybir

F32 = mybir.dt.float32
F32R = mybir.dt.float32r
I32 = mybir.dt.int32
ALU = mybir.AluOpType
ACT = mybir.ActivationFunctionType

P = 128
D = 128
GROUP = 2 * P
ONEHOT = 6
QUAD = 4
BLOCK = 32
BANK = 512


def feature_order(rows):
    small = sorted(sorted(range(len(rows)), key=lambda f: (rows[f], f))[:ONEHOT])
    return [f for f in range(len(rows)) if f not in small], small


def pair_chunks(slots):
    return -(-(slots - 1) // QUAD)


def build_tower(nc, dense, ids, onehot_ids, tables, w1, b1, w2, b2, w3, y_out):
    SAMPLES = dense.shape[1]
    GROUPS = SAMPLES // GROUP
    NF = len(tables)
    SLOTS = NF + 1
    gathered_f, onehot_f = feature_order([t.shape[0] for t in tables])
    NX = len(gathered_f)
    PER = BANK // P
    NT = -(-NX // PER)
    assert NX == NT * PER
    NB = 2 * NT
    TABLE_ROWS = tables[onehot_f[0]].shape[0]
    assert all(tables[f].shape[0] == TABLE_ROWS for f in onehot_f)
    RC = 8
    RP = TABLE_ROWS // RC
    assert RP * RC == TABLE_ROWS and RP <= P
    HALVES = 2 * len(onehot_f)
    RING = 3
    NO = -(-len(onehot_f) // 2)
    PC = pair_chunks(SLOTS)
    KC = PC + 1
    FULL, HALF = PC - 1, P // 2
    assert (SLOTS - 1) - QUAD * FULL <= QUAD // 2
    H1, H2 = w1.shape[2], w2.shape[1]
    M1, M2 = H1 // P, H2 // P
    NG = SLOTS - 1
    NF_ROWS = SLOTS - 1
    RUNS = P // QUAD
    LHS = BLOCK * (QUAD - 1) + NF_ROWS
    PARTS = 4
    ACC_READY = M1 // 2 + 2
    IP = RUNS // PARTS
    assert M1 == 4 and M2 == 2 and HALVES % RING == 0 and IP * QUAD * NG <= 2 * BANK and BLOCK * QUAD == P

    STEPS = [("old", 1), ("turn", 0), ("split", 0), ("old", 2), ("old", 3), ("turn", 1),
             ("split", 1), ("onehot", 0), ("turn", 2), ("onehot", 1), ("turn", 3), ("layer1", 0),
             ("layer1", 1), ("turn", 4), ("onehot", 2), ("turn", 5), ("layer1", 2), ("turn", 6),
             ("layer1", 3), ("turn", 7), ("new", 0), ("new", 1), ("turn", 8), ("layer2", 0),
             ("new", 2), ("layer2", 1), ("turn", 9), ("new", 3), ("late", 0), ("layer3", 0)]
    STEPS_FIRST = [("piece", 0), ("piece", 1), ("piece", 2), ("piece", 3), ("piece", 4), ("onehot", 0),
                   ("turn", 0), ("piece", 5), ("turn", 1), ("piece", 6), ("onehot", 1), ("piece", 7),
                   ("turn", 2), ("piece", 8), ("onehot", 2), ("turn", 3), ("piece", 9),
                   ("piece", 10), ("turn", 4), ("new", 0), ("new", 1), ("turn", 5), ("new", 2),
                   ("turn", 6), ("new", 3), ("turn", 7), ("turn", 8), ("turn", 9), ("late", 0)]
    STEPS_LAST = [("old", 1), ("split", 0), ("old", 2), ("old", 3), ("split", 1), ("layer1", 0),
                  ("layer1", 1), ("layer1", 2), ("layer1", 3), ("layer2", 0), ("layer2", 1), ("layer3", 0)]
    assert NB == 10 and NO == 3

    def uses(steps):
        return [(kind, i if kind == "onehot" else i // 2) for kind, i in steps
                if kind in ("onehot", "layer3") or (kind in ("layer1", "layer2") and i % 2)]

    USES_FIRST, USES, USES_LAST = uses(STEPS_FIRST), uses(STEPS), uses(STEPS_LAST)
    assert len(USES_FIRST) % 2 == len(USES) % 2

    def acc_use(g, kind, i):
        which = (kind, i if kind == "onehot" else i // 2)
        if isinstance(g, int) and g == 0:
            return USES_FIRST.index(which)
        order = USES_LAST if isinstance(g, int) and g == GROUPS else USES
        return g * len(USES) + (order.index(which) - len(USES) + len(USES_FIRST))

    def acc_place(g, kind, i):
        order = USES
        if isinstance(g, int) and g in (0, GROUPS):
            order = USES_FIRST if g == 0 else USES_LAST
        return order.index((kind, i if kind == "onehot" else i // 2))

    def acc_bank(g, kind, i):
        return acc_place(g, kind, i) % 2

    def acc_distance(g, kind, i):
        place = acc_place(g, kind, i)
        return 2 if place >= 2 or len(USES) % 2 == 0 else 1 + 2 * place

    with ExitStack() as ctx:
        def sb(name, shape, dt=F32):
            return ctx.enter_context(nc.sbuf_tensor(name, shape, dt))

        def psum(name, shape):
            return ctx.enter_context(nc.psum_tensor(name, shape, F32))

        def sem(name):
            return ctx.enter_context(nc.semaphore(name))

        idx = sb("idx", [P, 2, NF], I32)
        rows = sb("rows", [P, 2, NX, D])
        dense_t = sb("dense_t", [P, GROUP])
        feats = sb("feats", [P, 2, RUNS, QUAD, BLOCK])
        onehot_idx = sb("onehot_idx", [P, len(onehot_f), GROUP], I32)
        first_row = sb("first_row", [P, 1])
        first_row_i = sb("first_row_i", [P, 1], I32)
        onehot = sb("onehot", [P, RING, RC // 2, GROUP], F32R)
        table_high = sb("table_high", [P, len(onehot_f), RC, D], F32R)
        table_low = sb("table_low", [P, len(onehot_f), RC, D], F32R)
        w1_high = sb("w1_high", [P, KC, H1], F32R)
        w1_low = sb("w1_low", [P, KC, H1], F32R)
        w2_high = sb("w2_high", [P, M1, H2], F32R)
        w2_low = sb("w2_low", [P, M1, H2], F32R)
        w3_sb = sb("w3_sb", [P, M2])
        b1_sb = sb("b1_sb", [P, M1])
        b2_sb = sb("b2_sb", [P, M2])
        pairs = sb("pairs", [P, PC, GROUP])
        z_high = sb("z_high", [P, KC, GROUP], F32R)
        z_low = sb("z_low", [P, KC, GROUP], F32R)
        h1 = sb("h1", [P, M1, GROUP])
        h1_high = sb("h1_high", [P, M1, GROUP], F32R)
        h1_low = sb("h1_low", [P, M1, GROUP], F32R)
        h2 = sb("h2", [P, M2, GROUP])
        y_sb = sb("y_sb", [1, GROUP])
        ident = sb("ident", [P, P])
        stage = sb("stage", [P, RC * D])
        in_rows = [rows[:, 1, NX - k * RC:NX - k * RC + RC, :].rearrange("p x d -> p (x d)") for k in (2, 1)]
        in_h1 = h1[:, :, :].rearrange("p m n -> p (m n)")
        in_pairs = pairs[:, 0:PC // 2 + 1, :].rearrange("p c n -> p (c n)")
        STAGE = 2 * (in_rows + [in_h1, in_pairs, stage[:, :]]) + [in_h1]
        BEFORE = {5: 0, 6: 1, 7: 2, 8: 3, 9: 4, 10: 7}
        LAST_IN_ROWS, LAST_IN_PAIRS = 6, 8
        second = h2[:, :, :].rearrange("p m n -> p (m n)")

        turned = psum("turned", [P, 2, BANK])
        gram = psum("gram", [P, 2, 2, BANK])
        acc = psum("acc", [P, 2, BANK])

        idx_in = [sem(f"idx_in{t}") for t in range(2)]
        dense_in = sem("dense_in")
        gathered = [[sem(f"gathered{t}_{q}") for q in range(NT)] for t in range(2)]
        onehot_idx_in = sem("onehot_idx_in")
        small_in = sem("small_in")
        second_in = sem("second_in")
        second_added = sem("second_added")
        piece_high_ready = sem("piece_high_ready")
        piece_ready = sem("piece_ready")
        ident_zero = sem("ident_zero")
        ident_ready = sem("ident_ready")
        numbers_made = sem("numbers_made")
        numbers_ready = sem("numbers_ready")
        cleared = sem("cleared")
        turned_ready = sem("turned_ready")
        turned_out = sem("turned_out")
        onehot_ready = sem("onehot_ready")
        onehot_used = sem("onehot_used")
        acc_ready = sem("acc_ready")
        acc_out = sem("acc_out")
        gram_ready = sem("gram_ready")
        gram_out_even = sem("gram_out_even")
        gram_out_odd = sem("gram_out_odd")
        rest_even = sem("rest_even")
        rest_odd = sem("rest_odd")
        idx_relative = sem("idx_relative")
        dense_in_feats = sem("dense_in_feats")
        dense_high_ready = sem("dense_high_ready")
        dense_ready = sem("dense_ready")
        z_high_ready = sem("z_high_ready")
        z_ready = sem("z_ready")
        h1_even_out = sem("h1_even_out")
        h1_ready = sem("h1_ready")
        h2_even_out = sem("h2_even_out")
        y_stored = sem("y_stored")
        pool_passed = sem("pool_passed")
        sp_passed = sem("sp_passed")
        act_passed = sem("act_passed")

        pieces = []
        for n, f in enumerate(onehot_f):
            pieces.append((tables[f].rearrange("(p c) d -> p c d", c=RC),
                           table_high[0:RP, n, :, :], table_low[0:RP, n, :, :]))
        for c in range(0, KC, 2):
            e = min(c + 2, KC)
            pieces.append((w1[c:e].rearrange("c p n -> p c n"), w1_high[:, c:e, :], w1_low[:, c:e, :]))
        DENSE_PIECE = len(pieces) - 1
        pieces.append((w2.rearrange("(c p) n -> p c n", p=P), w2_high[:, :, :], w2_low[:, :, :]))
        assert len(STAGE) == len(pieces)

        def staged(n):
            p, a, b = pieces[n][1].shape
            return STAGE[n][0:p, 0:a * b].rearrange("p (a b) -> p a b", b=b)

        piece_in = [sem(f"piece_in{n}") for n in range(len(pieces))]

        def slot_columns(t, first, count):
            whole = feats[:, t, :, :, :].rearrange("p i s x -> p x s i")
            return whole[:, first:first + count, :, :]

        def by_run(v):
            return v.rearrange("p x (s i) -> p x s i", i=RUNS)

        def gram_block(k, s, j):
            n = len(range(j, NG, QUAD))
            v = gram[BLOCK * s:BLOCK * s + NF_ROWS, k, :, 0:(IP // 2) * QUAD * NG]
            v = v.rearrange("p a (i x) -> p a i x", x=QUAD * NG)
            return v[:, :, :, s * NG + j:s * NG + j + QUAD * (n - 1) + 1:QUAD], n

        def pair_block(t, part, s, j, n):
            first = t * P + s * RUNS + part * IP
            v = pairs[BLOCK * j:BLOCK * j + NF_ROWS, 0:n, first:first + IP]
            return v.rearrange("p c (a i) -> p a i c", a=2)

        def last_group(g):
            return isinstance(g, int) and g == GROUPS

        def acc_done(g, kind, m):
            before = g * ACC_READY - ACC_READY
            if last_group(g):
                return before + {"layer1": m + 1, "layer2": M1 + m + 1, "layer3": M1 + M2 + 1}[kind]
            return before + {"layer1": m // 2 + 1, "layer2": M1 // 2 + 1, "layer3": ACC_READY}[kind]

        def layer1_out(g, m):
            if last_group(g) and m % 2:
                return gram[:, 0, m // 2, 0:GROUP]
            return acc[:, acc_bank(g, "layer1", m), (m % 2) * GROUP:(m % 2 + 1) * GROUP]

        def layer2_out(g, m):
            if last_group(g) and m % 2:
                return gram[:, 1, 0, 0:GROUP]
            return acc[:, acc_bank(g, "layer2", m), m * GROUP:(m + 1) * GROUP]

        block = ctx.enter_context(nc.Block())

        @block.sync
        def _(sp):
            def load_piece(n):
                if n in BEFORE:
                    sp.wait_ge(piece_ready, BEFORE[n] + 1)
                sp.dma_start(staged(n), pieces[n][0]).then_inc(piece_in[n], 16)

            def load_tile(g, t):
                at = g * GROUP + t * P
                if not (isinstance(g, int) and g == 0):
                    at = sp.snap(at)
                    for q in range(NT):
                        sp.wait_ge(gathered[t][q], g * (16 * PER))
                        sp.sem_inc(sp_passed, 1)
                sp.dma_start(idx[:, t, :], ids[bass.ds(at, P), :]).then_inc(idx_in[t], 16)

            def load_dense(g):
                at = g * GROUP
                if not (isinstance(g, int) and g == 0):
                    at = sp.snap(at)
                    sp.wait_ge(dense_ready, g)
                    sp.sem_inc(sp_passed, 1)
                sp.dma_start(dense_t[:, :], dense[:, bass.ds(at, GROUP)]).then_inc(dense_in, 16)

            def load_onehot_idx(g):
                at = g * GROUP
                if not (isinstance(g, int) and g == 0):
                    at = sp.snap(at)
                    sp.wait_ge(onehot_ready, g * HALVES)
                    sp.sem_inc(sp_passed, 1)
                src = onehot_ids[:, bass.ds(at, GROUP)].rearrange("(o k) b -> o k b", o=1)
                sp.dma_start(onehot_idx[:, :, :], src.to_broadcast([P, len(onehot_f), GROUP]))\
                  .then_inc(onehot_idx_in, 16)

            load_tile(0, 0)
            load_onehot_idx(0)
            for n in range(2):
                load_piece(n)
            load_tile(0, 1)
            for n in range(2, len(onehot_f)):
                load_piece(n)
            load_dense(0)
            sp.dma_start(second, w1[KC]).then_inc(second_in, 16)
            for n in range(len(onehot_f), len(pieces)):
                load_piece(n)
            sp.dma_start(b1_sb[:, :], b1).then_inc(small_in, 16)
            sp.dma_start(b2_sb[:, :], b2).then_inc(small_in, 16)
            sp.dma_start(w3_sb[:, :], w3).then_inc(small_in, 16)
            with sp.Fori(1, GROUPS) as g:
                load_tile(g, 0)
                load_onehot_idx(g)
                load_tile(g, 1)
                load_dense(g)

        @block.gpsimd
        def _(pool):
            pool.memset(ident[:, :], 0.0).then_inc(ident_zero, 1)
            pool.iota(first_row_i[:, :], pattern=[[0, 1]], base=0, channel_multiplier=RC)\
                .then_inc(numbers_made, 1)
            pool.wait_ge(ident_zero, 1)
            pool.affine_select(out=ident[:, :], in_=ident[:, :], compare_op=ALU.not_equal, fill=1.0,
                               base=0, pattern=[[-1, P]], channel_multiplier=1).then_inc(ident_ready, 1)

            def gather_group(g, first):
                for t in range(2):
                    pool.wait_ge(idx_in[t], g * 16 + 16)
                    if first and t == 1:
                        pool.wait_ge(piece_ready, LAST_IN_ROWS + 1)
                    for q in range(NT):
                        if not first:
                            pool.wait_ge(turned_ready, g * NB + (t * NT + q + 1 - NB))
                            pool.sem_inc(pool_passed, 1)
                        for x in range(q * PER, (q + 1) * PER):
                            f = gathered_f[x]
                            pool.indirect_dma_start(
                                out=rows[:, t, x, :], out_offset=None, in_=tables[f],
                                in_offset=bass.IndirectOffsetOnAxis(ap=idx[:, t, f:f + 1], axis=0),
                            ).then_inc(gathered[t][q], 16)

            gather_group(0, True)
            with pool.Fori(1, GROUPS) as g:
                gather_group(g, False)

        @block.tensor
        def _(pe):
            def transposes(g, b, first):
                t, q = divmod(b, NT)
                pe.wait_ge(gathered[t][q], g * (16 * PER) + 16 * PER)
                if not (first and b < 2):
                    pe.wait_ge(turned_out, g * NB + (b - 1))
                for k in range(PER):
                    last = pe.transpose(turned[:, b % 2, k * P:(k + 1) * P], rows[:, t, q * PER + k, :],
                                        ident[:, :])
                last.then_inc(turned_ready, 1)

            def acc_free(g, kind, i, first):
                use = acc_use(g, kind, i)
                if not (first and use < 2):
                    pe.wait_ge(acc_out, use - acc_distance(g, kind, i) + 1)

            def onehot_bank(g, i, first):
                acc_free(g, "onehot", i, first)
                for n in range(2 * i, min(2 * i + 2, len(onehot_f))):
                    out = acc[:, acc_bank(g, "onehot", i), (n % 2) * GROUP:(n % 2 + 1) * GROUP]
                    if first:
                        pe.wait_ge(piece_ready, n + 1)
                    for h in range(2):
                        pe.wait_ge(onehot_ready, g * HALVES + (2 * n + h + 1))
                        for c in range(RC // 2):
                            for part, table in enumerate((table_high, table_low)):
                                last = pe.matmul(out, lhsT=table[0:RP, n, h * (RC // 2) + c, :],
                                                 rhs=onehot[0:RP, (2 * n + h) % RING, c, :],
                                                 start=(h == 0 and c == 0 and part == 0),
                                                 stop=(h == 1 and c == RC // 2 - 1 and part == 1))
                        last.then_inc(onehot_used, 1)

            def gram_part(g, t, part, first, last_tile=False):
                if part == 0:
                    pe.wait_ge(turned_out, g * NB + (t + 1) * NT)
                    pe.wait_ge(dense_in_feats, g + 1)
                    if t == 0:
                        pe.wait_ge(acc_out, acc_use(g, "onehot", NO - 1) + 1)
                k = part % 2
                if not (first and t == 0 and part < 2):
                    done = g * PARTS + (t * (PARTS // 2) + part // 2)
                    pe.wait_ge(gram_out_odd if k else gram_out_even, done)
                if last_tile and part == 3:
                    pe.wait_ge(rest_odd, 1)
                for i in range(IP):
                    a, b = divmod(i, IP // 2)
                    last = pe.matmul(gram[0:LHS, k, a, b * QUAD * NG:(b + 1) * QUAD * NG],
                                     lhsT=feats[:, t, part * IP + i, :, :].rearrange("p s x -> p (s x)")[:, 0:LHS],
                                     rhs=feats[:, t, part * IP + i, :, 1:SLOTS], start=True, stop=True)
                last.then_inc(gram_ready, 1)

            def layer1_dense(g, m):
                block = slice(m * P, (m + 1) * P)
                for n, (weights, z) in enumerate(((w1_high, z_high), (w1_low, z_high), (w1_high, z_low))):
                    pe.matmul(layer1_out(g, m), lhsT=weights[:, PC, block], rhs=z[:, PC, :],
                              start=(n == 0), stop=False)

            def layer1_high(g, m):
                block = slice(m * P, (m + 1) * P)
                for c in range(FULL):
                    if m == 0 and c % (FULL // 2) == 0:
                        pe.wait_ge(z_high_ready, g * 6 - (2 if c == 0 else 1))
                    for weights in (w1_high, w1_low):
                        pe.matmul(layer1_out(g, m), lhsT=weights[:, c, block], rhs=z_high[:, c, :],
                                  start=False, stop=False)

            def layer1_low(g, m):
                block = slice(m * P, (m + 1) * P)
                if m == 0:
                    pe.wait_ge(z_ready, g * 2)
                for weights in (w1_high, w1_low):
                    pe.matmul(layer1_out(g, m), lhsT=weights[:, FULL, block], rhs=z_high[:, FULL, :],
                              start=False, stop=False)
                for c in range(FULL):
                    last = pe.matmul(layer1_out(g, m), lhsT=w1_high[:, c, block], rhs=z_low[:, c, :],
                                     start=False, stop=(c == FULL - 1))
                if m % 2 or last_group(g):
                    last.then_inc(acc_ready, 1)

            def layer1(g, m):
                if m % 2 == 0:
                    acc_free(g, "layer1", m, False)
                if m == 0:
                    pe.wait_ge(dense_ready, g)
                layer1_dense(g, m)
                layer1_high(g, m)
                layer1_low(g, m)

            def layer1_last(g):
                acc_free(g, "layer1", 0, False)
                acc_free(g, "layer1", 2, False)
                pe.wait_ge(gram_out_even, GROUPS * PARTS)
                pe.wait_ge(rest_even, 1)
                pe.wait_ge(dense_ready, g)
                for m in range(M1):
                    layer1_dense(g, m)
                layer1_high(g, 0)
                layer1_high(g, 1)
                layer1_low(g, 0)
                layer1_low(g, 1)
                for m in range(2, M1):
                    layer1_high(g, m)
                    layer1_low(g, m)

            def layer2(g, m):
                if m == 0:
                    acc_free(g, "layer2", 0, False)
                out = layer2_out(g, m)
                for c in range(M1):
                    if m == 0:
                        pe.wait_ge(h1_ready, g * M1 + (c + 1 - M1))
                    for a, b in ((w2_high, h1_high), (w2_high, h1_low), (w2_low, h1_high)):
                        last = pe.matmul(out, lhsT=a[:, c, m * P:(m + 1) * P], rhs=b[:, c, :],
                                         start=(c == 0 and a is w2_high and b is h1_high),
                                         stop=(c == M1 - 1 and a is w2_low))
                if m == M2 - 1 or last_group(g):
                    last.then_inc(acc_ready, 1)

            def layer3(g):
                for c in range(M2):
                    if c < M2 - 1:
                        pe.wait_ge(h2_even_out, g)
                    else:
                        pe.wait_ge(acc_out, acc_use(g, "layer2", c) + 1)
                    last = pe.matmul(acc[0:1, acc_bank(g, "layer3", 0), 0:GROUP], lhsT=w3_sb[:, c:c + 1],
                                     rhs=h2[:, c, :], start=(c == 0), stop=(c == M2 - 1))
                last.then_inc(acc_ready, 1)

            def step(g, what, first=False):
                kind, i = what
                if kind == "turn":
                    transposes(g, i, first)
                elif kind == "old":
                    gram_part(g - 1, 1, i, False, last_group(g))
                elif kind == "new":
                    gram_part(g, 0, i, first)
                elif kind == "late":
                    gram_part(g, 1, i, False)
                elif kind == "onehot":
                    onehot_bank(g, i, first)
                elif kind == "layer1" and not last_group(g):
                    layer1(g, i)
                elif kind == "layer1" and i == 0:
                    layer1_last(g)
                elif kind == "layer2":
                    layer2(g, i)
                elif kind == "layer3":
                    layer3(g)

            pe.wait_ge(ident_ready, 1)
            pe.wait_ge(cleared, 1)
            for what in STEPS_FIRST:
                step(0, what, True)
            pe.wait_ge(piece_ready, len(pieces))
            pe.wait_ge(small_in, 48)
            with pe.Fori(1, GROUPS) as g:
                for what in STEPS:
                    step(g, what)
            for what in STEPS_LAST:
                step(GROUPS, what)

        @block.scalar
        def _(act):
            def piece_high(n):
                high = pieces[n][1]
                act.wait_ge(piece_in[n], 16)
                if n == DENSE_PIECE:
                    act.wait_ge(second_added, 1)
                act.copy(high, staged(n)).then_inc(piece_high_ready, 1)

            def turned_move(g, b, first):
                t, q = divmod(b, NT)
                act.wait_ge(turned_ready, g * NB + (b + 1))
                if not first:
                    if q == 0:
                        act.wait_ge(gram_ready, g * (2 * PARTS) + (t - 1) * PARTS)
                act.copy(slot_columns(t, 1 + q * PER, PER),
                         by_run(turned[:, b % 2, :].rearrange("p (x b) -> p x b", b=P)))\
                   .then_inc(turned_out, 1)

            def onehot_move(g, i, first):
                ns = range(2 * i, min(2 * i + 2, len(onehot_f)))
                act.wait_ge(onehot_used, g * HALVES + (2 * ns[-1] + 2))
                if not first and i == 0:
                    act.wait_ge(gram_ready, g * (2 * PARTS))
                src = acc[:, acc_bank(g, "onehot", i), 0:len(ns) * GROUP].rearrange("p (n b) -> p n b", n=len(ns))
                for t in range(2):
                    last = act.copy(slot_columns(t, 1 + NX + ns[0], len(ns)), by_run(src[:, :, t * P:(t + 1) * P]))
                last.then_inc(acc_out, 1)

            def gram_move(g, t, part, first, half=False):
                act.wait_ge(gram_ready, g * (2 * PARTS) + (t * PARTS + part + 1))
                if first and part == 1:
                    act.wait_ge(cleared, 2)
                for s in range(QUAD // 2 if half else QUAD):
                    for j in range(QUAD):
                        src, n = gram_block(part % 2, s, j)
                        last = act.copy(pair_block(t, part, s, j, n), src)
                last.then_inc(gram_out_odd if part % 2 else rest_even, 1)

            def relu1(g, half):
                for m in (2 * half, 2 * half + 1):
                    act.wait_ge(acc_ready, acc_done(g, "layer1", m))
                    src = layer1_out(g, m)
                    act.activation(h1[:, m, :], src, ACT.Relu, bias=b1_sb[:, m:m + 1])
                    last = act.activation(h1_high[:, m, :], src, ACT.Relu, bias=b1_sb[:, m:m + 1])
                    if m % 2 == 0:
                        last.then_inc(h1_even_out, 1)
                last.then_inc(acc_out, 1)

            def relu2(g):
                for m in range(M2):
                    act.wait_ge(acc_ready, acc_done(g, "layer2", m))
                    last = act.activation(h2[:, m, :], layer2_out(g, m), ACT.Relu, bias=b2_sb[:, m:m + 1])
                    if m % 2 == 0:
                        last.then_inc(h2_even_out, 1)
                last.then_inc(acc_out, 1)

            def y_move(g, first):
                act.wait_ge(acc_ready, acc_done(g, "layer3", 0))
                if not first:
                    act.wait_ge(y_stored, g * 16 - 16)
                act.copy(y_sb[:, :], acc[0:1, acc_bank(g, "layer3", 0), 0:GROUP]).then_inc(acc_out, 1)
                at = (g - 1) * GROUP if isinstance(g, int) else act.snap((g - 1) * GROUP)
                act.wait_ge(acc_out, acc_use(g, "layer3", 0) + 1)
                act.sem_inc(act_passed, 1)
                act.dma_start(y_out[bass.ds(at, GROUP), :].rearrange("b o -> o b"), y_sb[:, :])\
                   .then_inc(y_stored, 16)

            def split_pairs(g, t, last_group):
                if last_group and t == 1:
                    act.wait_ge(rest_even, 1)
                    act.wait_ge(rest_odd, 2)
                act.wait_ge(gram_out_even, g * PARTS + (t + 1) * (PARTS // 2))
                act.wait_ge(gram_out_odd, g * PARTS + (t + 1) * (PARTS // 2))
                mine = slice(t * P, (t + 1) * P)
                for c in range(0, FULL, FULL // 2):
                    cs = slice(c, c + FULL // 2)
                    act.copy(z_high[:, cs, mine], pairs[:, cs, mine]).then_inc(z_high_ready, 1)
                act.copy(z_high[0:HALF, FULL, mine], pairs[0:HALF, FULL, mine]).then_inc(z_high_ready, 1)

            def step(g, what, first=False):
                kind, i = what
                if kind == "turn":
                    turned_move(g, i, first)
                elif kind == "split":
                    split_pairs(g - 1, i, last_group(g))
                elif kind == "piece":
                    piece_high(i)
                elif kind == "old" and (i % 2 or last_group(g)):
                    gram_move(g - 1, 1, i, g_is(g, 1), last_group(g))
                elif kind == "new" and i % 2:
                    gram_move(g, 0, i, first)
                elif kind == "onehot":
                    onehot_move(g, i, first)
                elif kind == "layer1" and i % 2:
                    relu1(g, i // 2)
                elif kind == "layer2" and i == M2 - 1:
                    relu2(g)
                elif kind == "layer3":
                    y_move(g, g_is(g, 1))

            def g_is(g, n):
                return isinstance(g, int) and g == n

            for what in STEPS_FIRST:
                step(0, what, True)
            act.wait_ge(small_in, 48)
            for what in STEPS:
                step(1, what)
            with act.Fori(2, GROUPS) as g:
                for what in STEPS:
                    step(g, what)
            for what in STEPS_LAST:
                step(GROUPS, what)
            act.wait_ge(y_stored, 16 * GROUPS)

        @block.vector
        def _(dve):
            dve.memset(feats[:, :, :, :, SLOTS:BLOCK], 0.0).then_inc(cleared, 1)
            dve.wait_ge(numbers_made, 1)
            dve.tensor_copy(first_row[:, :], first_row_i[:, :]).then_inc(numbers_ready, 1)
            dve.wait_ge(numbers_ready, 1)

            def piece_low(n):
                _, high, low = pieces[n]
                if n == DENSE_PIECE:
                    dve.wait_ge(piece_in[n], 16)
                    dve.wait_ge(second_in, 16)
                    last = staged(n)[:, high.shape[1] - 1, :]
                    dve.tensor_add(last, last, second).then_inc(second_added, 1)
                dve.wait_ge(piece_high_ready, n + 1)
                dve.tensor_sub(low, staged(n), high).then_inc(piece_ready, 1)

            def half_table(g, n, first):
                if n == 0:
                    dve.wait_ge(onehot_idx_in, g * 16 + 16)
                    dve.tensor_scalar(onehot_idx[:, :, :], onehot_idx[:, :, :], first_row[:, 0:1], None,
                                      ALU.subtract).then_inc(idx_relative, 1)
                    dve.wait_ge(idx_relative, g + 1)
                if not (first and n < RING):
                    dve.wait_ge(onehot_used, g * HALVES + (n - RING + 1))
                for c in range(RC // 2):
                    k = (n % 2) * (RC // 2) + c
                    last = dve.tensor_scalar(onehot[:, n % RING, c, :], onehot_idx[:, n // 2, :],
                                             float(k), None, ALU.is_equal)
                last.then_inc(onehot_ready, 1)

            def gram_move(g, t, part, half=False):
                dve.wait_ge(gram_ready, g * (2 * PARTS) + (t * PARTS + part + 1))
                for s in range(QUAD // 2 if half else 0, QUAD):
                    for j in range(QUAD):
                        src, n = gram_block(part % 2, s, j)
                        last = dve.tensor_copy(pair_block(t, part, s, j, n), src)
                last.then_inc(rest_odd if part % 2 else gram_out_even, 1)

            def layer1_done(g):
                return g * ACC_READY - 2

            def dense_to_feats(g):
                dve.wait_ge(dense_in, g * 16 + 16)
                if not (isinstance(g, int) and g == 0):
                    dve.wait_ge(gram_ready, g * (2 * PARTS))
                dve.tensor_copy(feats[:, :, :, :, 0].rearrange("p t i s -> p t s i"),
                                dense_t[:, :].rearrange("p (t s i) -> p t s i", t=2, i=RUNS))\
                   .then_inc(dense_in_feats, 1)

            def split_dense(g, first):
                if first:
                    dve.wait_ge(dense_in, 16)
                else:
                    dve.wait_ge(acc_ready, layer1_done(g))
                dve.tensor_copy(z_high[:, PC, :], dense_t[:, :]).then_inc(dense_high_ready, 1)
                dve.wait_ge(dense_high_ready, g + 1)
                dve.tensor_sub(z_low[:, PC, :], dense_t[:, :], z_high[:, PC, :]).then_inc(dense_ready, 1)

            def split_pairs(g, t):
                dve.wait_ge(z_high_ready, g * 6 + (t + 1) * 3)
                mine = slice(t * P, (t + 1) * P)
                dve.tensor_sub(z_low[:, 0:FULL, mine], pairs[:, 0:FULL, mine], z_high[:, 0:FULL, mine])
                dve.tensor_sub(z_high[HALF:P, FULL, mine], pairs[0:HALF, FULL, mine],
                               z_high[0:HALF, FULL, mine]).then_inc(z_ready, 1)

            def h1_split(g, m):
                if m % 2:
                    dve.wait_ge(acc_out, acc_use(g, "layer1", m) + 1)
                else:
                    dve.wait_ge(h1_even_out, g * (M1 // 2) + (m // 2 + 1 - M1 // 2))
                dve.tensor_sub(h1_low[:, m, :], h1[:, m, :], h1_high[:, m, :]).then_inc(h1_ready, 1)

            def step(g, what, first=False):
                kind, i = what
                if kind == "half":
                    half_table(g, i, first)
                elif kind == "next_half":
                    half_table(g + 1, i, False)
                elif kind == "piece":
                    piece_low(i)
                elif kind == "clear_pairs":
                    dve.wait_ge(piece_ready, LAST_IN_PAIRS + 1)
                    dve.memset(pairs[:, :, :], 0.0).then_inc(cleared, 1)
                    dve.wait_ge(cleared, 2)
                elif kind == "old":
                    gram_move(g - 1, 1, i, last_group(g))
                elif kind == "new":
                    gram_move(g, 0, i)
                elif kind == "late":
                    gram_move(g, 1, i)
                elif kind == "split":
                    split_pairs(g - 1, i)
                elif kind == "dense_feats":
                    dense_to_feats(g)
                elif kind == "dense":
                    split_dense(g, first)
                elif kind == "h1":
                    h1_split(g, i)

            OWN_FIRST = [("half", 0), ("piece", 0), ("half", 1), ("piece", 1), ("half", 2), ("piece", 2),
                         ("half", 3), ("half", 4), ("piece", 3), ("half", 5), ("piece", 4), ("half", 6),
                         ("half", 7), ("piece", 5), ("half", 8), ("piece", 6), ("half", 9), ("half", 10),
                         ("half", 11), ("dense_feats", 0), ("piece", 7), ("piece", 8), ("clear_pairs", 0), ("piece", 9),
                         ("piece", 10), ("new", 0), ("new", 2), ("dense", 0),
                         ("next_half", 0), ("next_half", 1), ("next_half", 2), ("late", 0)]
            OWN = [("old", 2), ("split", 0), ("half", 3), ("half", 4), ("half", 5), ("half", 6),
                   ("split", 1), ("half", 7), ("half", 8), ("half", 9), ("half", 10), ("half", 11),
                   ("dense_feats", 0), ("h1", 0), ("h1", 1), ("h1", 2), ("h1", 3), ("new", 0), ("dense", 0),
                   ("next_half", 0), ("new", 2), ("next_half", 1), ("late", 0), ("next_half", 2)]
            OWN_END = [what for what in OWN if what[0] != "next_half"]
            OWN_LAST = [("old", 1), ("old", 2), ("old", 3), ("split", 0), ("split", 1), ("h1", 0), ("h1", 1), ("h1", 2), ("h1", 3)]
            for what in OWN_FIRST:
                step(0, what, True)
            with dve.Fori(1, GROUPS - 1) as g:
                for what in OWN:
                    step(g, what)
            for what in OWN_END:
                step(GROUPS - 1, what)
            for what in OWN_LAST:
                step(GROUPS, what)


def kernel(**inputs):
    import concourse.bacc as bacc
    from concourse.bass_utils import run_bass_kernel_spmd

    tables = [np.ascontiguousarray(inputs[f"tbl_{f}"]) for f in range(26)]
    gathered_f, onehot_f = feature_order([t.shape[0] for t in tables])
    slots = len(tables) + 1
    feature = [0] + [f + 1 for f in gathered_f + onehot_f]

    w1 = np.asarray(inputs["W_top1"])
    number = np.full((slots, slots), -1)
    number[np.triu_indices(slots, 1)] = np.arange(slots * (slots - 1) // 2)
    chunks = pair_chunks(slots)
    laid = np.zeros((chunks + 2, P, w1.shape[1]), w1.dtype)
    for g in range(1, slots):
        c, j = divmod(g - 1, QUAD)
        for f in range(g):
            a, b = sorted((feature[f], feature[g]))
            laid[c, BLOCK * j + f] = w1[D + number[a, b]]
    laid[chunks - 1, P // 2:] = laid[chunks - 1, :P // 2]
    laid[chunks] = w1[0:D]
    laid[chunks + 1] = w1[w1.shape[0] - D:]

    ids = np.ascontiguousarray(inputs["ids"])
    arrays = {
        "dense": np.ascontiguousarray(np.asarray(inputs["r_dense_features"]).T),
        "ids": ids,
        "onehot_ids": np.ascontiguousarray(ids.T[onehot_f]),
        "w1": laid,
        "b1": np.ascontiguousarray(np.asarray(inputs["b_top1"]).reshape(-1, P).T),
        "w2": np.ascontiguousarray(inputs["W_top2"]),
        "b2": np.ascontiguousarray(np.asarray(inputs["b_top2"]).reshape(-1, P).T),
        "w3": np.ascontiguousarray(np.asarray(inputs["W_top3"]).reshape(-1, P).T),
    }
    for f, t in enumerate(tables):
        arrays[f"tbl_{f}"] = t

    nc = bacc.Bacc("TRN2", target_bir_lowering=False, num_devices=1)
    aps = {n: nc.dram_tensor(n, a.shape, mybir.dt.from_np(a.dtype), kind="ExternalInput").ap()
           for n, a in arrays.items()}
    y = nc.dram_tensor("y", (ids.shape[0], 1), F32, kind="ExternalOutput").ap()
    build_tower(nc, aps["dense"], aps["ids"], aps["onehot_ids"], [aps[f"tbl_{f}"] for f in range(26)],
                aps["w1"], aps["b1"], aps["w2"], aps["b2"], aps["w3"], y)
    result = run_bass_kernel_spmd(nc, [arrays], core_ids=[0])
    return result.results[0]["y"]
```
